# Optimizing a Trainium2 kernel written in Bass

```python
import numpy as np
import jax
import jax.numpy as jnp

def _softmax(x, axis=-1):
    return jax.nn.softmax(x, axis=axis)

def _gelu(x):
    return jax.nn.gelu(x, approximate=True)

def _silu(x):
    return jax.nn.silu(x)

def _sigmoid(x):
    return jax.nn.sigmoid(x)

def _layernorm(x, axis=-1, eps=1e-05):
    m = jnp.mean(x, axis=axis, keepdims=True)
    v = jnp.var(x, axis=axis, keepdims=True)
    return (x - m) / jnp.sqrt(v + eps)

def _scatter_add(tgt, idx, src, axis=0):
    return tgt.at[idx].add(src)

def _segment_sum(src, seg, n):
    return jax.ops.segment_sum(src, seg, n)
kernel_name = 'mk_recurrent_d1_jaxref_r8_c731ec'

def setup_inputs(seed: int=0):
    np.random.seed(seed)
    _w = jnp.asarray

    def _L0_attn_setup():
        import jax, jax.numpy as jnp
        from jax import lax
        import numpy as np
        D = 128
        H = 16
        DK = D // 2 // H
        DV = D // H
        GATE_NORM = 16.0
        SCALE = DK ** (-0.5)
        EPS = 1e-05

        def _split_heads(x, dh):
            B, L, _ = x.shape
            return x.reshape(B, L, H, dh).transpose(0, 2, 1, 3)

        def _gla_scan(q, k, v, log_gate):
            B = q.shape[0]
            qt = jnp.moveaxis(q, 2, 0)
            kt = jnp.moveaxis(k, 2, 0)
            vt = jnp.moveaxis(v, 2, 0)
            gt = jnp.exp(jnp.moveaxis(log_gate, 2, 0))

            def step(state, inp):
                qq, kk, vv, gg = inp
                state = state * gg[..., None] + kk[..., :, None] * vv[..., None, :]
                out = jnp.einsum('bhd,bhde->bhe', qq, state)
                return (state, out)
            init = jnp.zeros((B, H, DK, DV), dtype=q.dtype)
            _, outs = lax.scan(step, init, (qt, kt, vt, gt))
            return jnp.moveaxis(outs, 0, 2)
        key = jax.random.key(seed)
        ks = jax.random.split(key, 10)
        s = 0.02
        return {'inputs': jax.random.normal(ks[0], (4, 512, D), dtype=jnp.float32), 'Wq': jax.random.normal(ks[1], (D, D // 2), dtype=jnp.float32) * s, 'Wk': jax.random.normal(ks[2], (D, D // 2), dtype=jnp.float32) * s, 'Wg1': jax.random.normal(ks[3], (D, 16), dtype=jnp.float32) * s, 'Wg2': jax.random.normal(ks[4], (16, D // 2), dtype=jnp.float32) * s, 'Wv': jax.random.normal(ks[5], (D, D), dtype=jnp.float32) * s, 'Wg': jax.random.normal(ks[6], (D, D), dtype=jnp.float32) * s, 'bg': jax.random.normal(ks[7], (D,), dtype=jnp.float32) * s, 'Wo': jax.random.normal(ks[8], (D, D), dtype=jnp.float32) * s}
    _L0_attn_in = _L0_attn_setup()

    def _L0_ffn_setup():
        import jax, jax.numpy as jnp
        import numpy as np
        HIDDEN = 128
        NUM_EXPERTS = 8
        TOP_K = 2
        key = jax.random.key(seed)
        k_x, k_r, k_w1, k_w2 = jax.random.split(key, 4)
        x = jax.random.normal(k_x, (4, 256, HIDDEN), dtype=jnp.float32)
        router_w = jax.random.normal(k_r, (NUM_EXPERTS, HIDDEN), dtype=jnp.float32) * HIDDEN ** (-0.5)
        w1 = jax.random.normal(k_w1, (NUM_EXPERTS, HIDDEN, 2 * HIDDEN), dtype=jnp.float32) * HIDDEN ** (-0.5)
        w2 = jax.random.normal(k_w2, (NUM_EXPERTS, 2 * HIDDEN, HIDDEN), dtype=jnp.float32) * (2 * HIDDEN) ** (-0.5)
        return {'x': x, 'router_w': router_w, 'w1': w1, 'w2': w2}
    _L0_ffn_in = _L0_ffn_setup()
    _d = {'L0_attn_inputs': _L0_attn_in['inputs'], 'L0_attn_Wq': _L0_attn_in['Wq'], 'L0_attn_Wk': _L0_attn_in['Wk'], 'L0_attn_Wg1': _L0_attn_in['Wg1'], 'L0_attn_Wg2': _L0_attn_in['Wg2'], 'L0_attn_Wv': _L0_attn_in['Wv'], 'L0_attn_Wg': _L0_attn_in['Wg'], 'L0_attn_bg': _L0_attn_in['bg'], 'L0_attn_Wo': _L0_attn_in['Wo'], 'L0_ffn_router_w': _L0_ffn_in['router_w'], 'L0_ffn_w1': _L0_ffn_in['w1'], 'L0_ffn_w2': _L0_ffn_in['w2']}
    _x0 = _d['L0_attn_inputs']
    _d['L0_attn_inputs'] = jax.random.normal(jax.random.fold_in(jax.random.key(seed), 1), (32, 256, 128), dtype=_x0.dtype)
    del _x0
    return _d

def reference(L0_attn_inputs, L0_attn_Wq, L0_attn_Wk, L0_attn_Wg1, L0_attn_Wg2, L0_attn_Wv, L0_attn_Wg, L0_attn_bg, L0_attn_Wo, L0_ffn_router_w, L0_ffn_w1, L0_ffn_w2):

    def _L0_attn_ref(inputs, Wq, Wk, Wg1, Wg2, Wv, Wg, bg, Wo):
        import jax, jax.numpy as jnp
        from jax import lax
        import numpy as np
        D = 128
        H = 16
        DK = D // 2 // H
        DV = D // H
        GATE_NORM = 16.0
        SCALE = DK ** (-0.5)
        EPS = 1e-05

        def _split_heads(x, dh):
            B, L, _ = x.shape
            return x.reshape(B, L, H, dh).transpose(0, 2, 1, 3)

        def _gla_scan(q, k, v, log_gate):
            B = q.shape[0]
            qt = jnp.moveaxis(q, 2, 0)
            kt = jnp.moveaxis(k, 2, 0)
            vt = jnp.moveaxis(v, 2, 0)
            gt = jnp.exp(jnp.moveaxis(log_gate, 2, 0))

            def step(state, inp):
                qq, kk, vv, gg = inp
                state = state * gg[..., None] + kk[..., :, None] * vv[..., None, :]
                out = jnp.einsum('bhd,bhde->bhe', qq, state)
                return (state, out)
            init = jnp.zeros((B, H, DK, DV), dtype=q.dtype)
            _, outs = lax.scan(step, init, (qt, kt, vt, gt))
            return jnp.moveaxis(outs, 0, 2)
        B, L, _ = inputs.shape
        q = _split_heads(inputs @ Wq, DK)
        k = _split_heads(inputs @ Wk * SCALE, DK)
        kg = _split_heads(inputs @ Wg1 @ Wg2, DK)
        v = _split_heads(inputs @ Wv, DV)
        gate = jax.nn.silu(inputs @ Wg + bg)
        log_gate = jax.nn.log_sigmoid(kg) / GATE_NORM
        o = _gla_scan(q, k, v, log_gate)
        mu = jnp.mean(o, axis=-1, keepdims=True)
        var = jnp.var(o, axis=-1, keepdims=True)
        o = (o - mu) * lax.rsqrt(var + EPS)
        o = o.transpose(0, 2, 1, 3).reshape(B, L, D)
        return gate * o @ Wo

    def _L0_ffn_ref(x, router_w, w1, w2):
        import jax, jax.numpy as jnp
        import numpy as np
        HIDDEN = 128
        NUM_EXPERTS = 8
        TOP_K = 2
        bsz, seq, hidden = x.shape
        tokens = x.reshape(-1, hidden)
        logits = tokens @ router_w.T
        topk_vals, topk_idx = jax.lax.top_k(logits, TOP_K)
        weights = jax.nn.softmax(topk_vals, axis=-1)
        h = jnp.einsum('td,edf->etf', tokens, w1)
        h = jax.nn.gelu(h, approximate=False)
        out_all = jnp.einsum('etf,efd->etd', h, w2)
        out_ted = jnp.transpose(out_all, (1, 0, 2))
        gathered = jnp.take_along_axis(out_ted, topk_idx[:, :, None], axis=1)
        output = jnp.sum(weights[:, :, None] * gathered, axis=1)
        return output.reshape(bsz, seq, hidden)
    x = L0_attn_inputs
    xn = _layernorm(x, axis=-1)
    s = _L0_attn_ref(xn, L0_attn_Wq, L0_attn_Wk, L0_attn_Wg1, L0_attn_Wg2, L0_attn_Wv, L0_attn_Wg, L0_attn_bg, L0_attn_Wo)
    g = _silu(_L0_ffn_ref(xn, L0_ffn_router_w, L0_ffn_w1, L0_ffn_w2))
    x = x + s * g
    return x

_drawn_inputs = setup_inputs


def setup_inputs(seed=0):
    import zlib

    import numpy as np

    out = dict(_drawn_inputs(seed))
    spreads = {}
    factors = {'L0_attn_Wq': 8.0,
     'L0_attn_Wk': 8.0,
     'L0_attn_Wg1': 8.0,
     'L0_attn_Wg2': 8.0,
     'L0_attn_Wv': 8.0,
     'L0_attn_Wg': 8.0,
     'L0_attn_bg': 8.0,
     'L0_attn_Wo': 8.0,
     'L0_ffn_router_w': 8.0,
     'L0_ffn_w1': 8.0,
     'L0_ffn_w2': 8.0}
    for name, (base, spread) in spreads.items():
        noise = np.random.default_rng([zlib.crc32(name.encode()), seed]).standard_normal(out[name].shape)
        drawn = base * np.exp(spread * noise) if base else spread * noise
        out[name] = jnp.asarray(drawn.astype(out[name].dtype))
    for name, factor in factors.items():
        out[name] = (out[name] * factor).astype(out[name].dtype)
    return out
```

```python
from contextlib import ExitStack

import concourse.bass as bass
from concourse import mybir

ALU = mybir.AluOpType
ACT = mybir.ActivationFunctionType
AX_X = mybir.AxisListType.X
F32 = mybir.dt.float32
F16 = mybir.dt.float16
U32 = mybir.dt.uint32

P = 128
TILES = 4
TOK = TILES * P
HEADS, DK, DV = 16, 4, 8
KW = HEADS * DK
SW = HEADS * DK * DV
EXPERTS = 8
FH = 2
GATE_NORM = 16.0
EPS = 1e-5
CQ, CK, CG, CR, CV, CO, CW = 0, 64, 128, 192, 200, 328, 456


def gla_moe_kernel(nc, x, Wq, Wk, Wg1, Wg2, Wv, Wg, bg, Wo, router_w, w1, w2, out):
    blocks = x.shape[0] * x.shape[1] // TOK
    assert blocks % 2 == 0 and blocks >= 6
    xb = x.rearrange("(n s) (c p) d -> n p (s c) d", s=2, p=P)
    ob = out.rearrange("(n s) (c p) d -> n p (s c) d", s=2, p=P)

    with ExitStack() as ctx:
        def sb(name, shape, dt=F32):
            return ctx.enter_context(nc.sbuf_tensor(name, shape, dt))

        def sem(name):
            return ctx.enter_context(nc.semaphore(name))

        def ps(name):
            return ctx.enter_context(nc.psum_tensor(name, [P, 512], F32))

        h_ps = [ps(f"h_ps{i}") for i in range(2)]
        y_ps = [ps(f"y_ps{i}") for i in range(2)]
        proj_ps = ps("proj_ps")
        state_ps = [ps(f"state_ps{i}") for i in range(2)]
        turn_ps = ps("turn_ps")

        wall = sb("wall", [P, CW])
        wall_hi, wall_lo = sb("wall_hi", [P, CW], F16), sb("wall_lo", [P, CW], F16)
        w1_raw, w2_raw = sb("w1_raw", [P, EXPERTS, 256]), sb("w2_raw", [P, EXPERTS, FH, P])
        w1_hi, w1_lo = sb("w1_hi", [P, EXPERTS, 256], F16), sb("w1_lo", [P, EXPERTS, 256], F16)
        w2_hi, w2_lo = sb("w2_hi", [P, EXPERTS, FH, P], F16), sb("w2_lo", [P, EXPERTS, FH, P], F16)
        wo = sb("wo", [P, P])
        wg1_in, wg2_in, router_in = sb("wg1_in", [P, 16]), sb("wg2_in", [16, KW]), sb("router_in", [EXPERTS, P])
        wg1_t = sb("wg1_t", [16, P])
        vmean = sb("vmean", [P, HEADS])
        bg_row, ones_row, bias = sb("bg_row", [1, P]), sb("ones_row", [1, P]), sb("bias", [P, P])
        ident, tri, first_half = sb("ident", [P, P]), sb("tri", [P, P]), sb("first_half", [P, P])
        second_half, last_row, decay_sum = sb("second_half", [P, P]), sb("last_row", [P, P]), sb("decay_sum", [P, P])
        expert_no = sb("expert_no", [P, TILES, EXPERTS])
        minus_half = sb("minus_half", [P, TILES * HEADS])

        x_in = [sb(f"x_in{i}", [P, TILES, P]) for i in range(2)]
        x_res = [sb(f"x_res{i}", [P, TILES, P]) for i in range(2)]
        y_out = [sb(f"y_out{i}", [P, TILES, P]) for i in range(2)]
        acc = [sb(f"acc{i}", [P, TILES, P]) for i in range(2)]
        attn = [sb(f"attn{i}", [P, TOK]) for i in range(2)]
        xt_hi = [sb(f"xt_hi{i}", [P, TOK], F16) for i in range(2)]
        xt_lo = [sb(f"xt_lo{i}", [P, TOK], F16) for i in range(2)]
        proj = [sb(f"proj{i}", [P, TILES, CW]) for i in range(2)]
        q_dec = [sb(f"q_dec{i}", [P, TILES, KW]) for i in range(2)]
        k_dec = [sb(f"k_dec{i}", [P, TILES, KW]) for i in range(2)]
        carry_dec = [sb(f"carry_dec{i}", [P, 2, KW]) for i in range(2)]
        mix = [sb(f"mix{i}", [P, TILES, EXPERTS]) for i in range(2)]
        stats, moments = sb("stats", [P, TILES, 6]), sb("moments", [P, TILES, 2])
        var_eps, rstd = sb("var_eps", [P, TILES]), sb("rstd", [P, TILES])
        xn = sb("xn", [P, TILES, P])
        kg_neg, kg_exp, kg_ln, log_g = (sb(n, [P, TILES, KW]) for n in ("kg_neg", "kg_exp", "kg_ln", "log_g"))
        e_pos, e_neg = sb("e_pos", [P, TILES, KW]), sb("e_neg", [P, TILES, KW])
        top, top_no = sb("top", [P, TILES, 8]), sb("top_no", [P, TILES, 8], U32)
        top_nof, gap, gap_t = sb("top_nof", [P, TILES, 8]), sb("gap", [P, TILES]), sb("gap_t", [P, TILES])
        p1, p2 = sb("p1", [P, TILES]), sb("p2", [P, TILES])
        pick1, pick2 = sb("pick1", [P, TILES, EXPERTS]), sb("pick2", [P, TILES, EXPERTS])
        kv = [sb(f"kv{i}", [P, SW]) for i in range(4)]
        carry = [sb(f"carry{i}", [P, SW]) for i in range(2)]
        qs = [sb(f"qs{i}", [P, SW]) for i in range(2)]
        o, o_sq = sb("o", [P, TILES, P]), sb("o_sq", [P, TILES, P])
        o_var, o_r = sb("o_var", [P, TILES * HEADS]), sb("o_r", [P, TILES * HEADS])
        o_ve = sb("o_ve", [P, TILES * HEADS])
        gate_in, gate_t, gate = (sb(n, [P, TILES, P]) for n in ("gate_in", "gate_t", "gate"))
        o_n, go = sb("o_n", [P, TILES, P]), sb("go", [P, TILES, P])
        go_t = sb("go_t", [P, TOK])
        sil_t, fin1, fin2 = (sb(n, [P, TOK]) for n in ("sil_t", "fin1", "fin2"))
        h_act = [sb(f"h_act{i}", [P, TOK]) for i in range(2)]
        h_hi = [sb(f"h_hi{i}", [P, TOK], F16) for i in range(4)]
        h_lo = [sb(f"h_lo{i}", [P, TOK], F16) for i in range(4)]

        w_small, w_moe, consts, ones_made = sem("w_small"), sem("w_moe"), sem("consts"), sem("ones_made")
        wprep, wprep_pe, split_done = sem("wprep"), sem("wprep_pe"), sem("split_done")
        dve_past, pool_past = sem("dve_past"), sem("pool_past")
        x_loaded = [sem(f"x_loaded{i}") for i in range(2)]
        res_loaded = [sem(f"res_loaded{i}") for i in range(2)]
        stored = [sem(f"stored{i}") for i in range(2)]
        ln_step, rstd_done, xn_done = sem("ln_step"), sem("rstd_done"), sem("xn_done")
        xt_turned, xt_hi_done, xt_lo_done = sem("xt_turned"), sem("xt_hi_done"), sem("xt_lo_done")
        proj_done, proj_copied = sem("proj_done"), sem("proj_copied")
        router_step, gap_done, gap_t_done, mix_done = sem("router_step"), sem("gap_done"), sem("gap_t_done"), sem("mix_done")
        kg_neg_done, kg_exp_done, kg_ln_done, log_g_done = (
            sem("kg_neg_done"), sem("kg_exp_done"), sem("kg_ln_done"), sem("log_g_done"))
        decay_done, e_done, qk_done = sem("decay_done"), sem("e_done"), sem("qk_done")
        kv_done, state_done, carry_done = sem("kv_done"), sem("state_done"), sem("carry_done")
        qs_done, o_done, o_sq_done, o_var_done, o_ve_done, o_r_done = (
            sem("qs_done"), sem("o_done"), sem("o_sq_done"), sem("o_var_done"), sem("o_ve_done"), sem("o_r_done"))
        gate_in_done, gate_t_done, gate_done, o_n_done, go_done = (
            sem("gate_in_done"), sem("gate_t_done"), sem("gate_done"), sem("o_n_done"), sem("go_done"))
        go_turned, go_t_done, wo_done, attn_done = sem("go_turned"), sem("go_t_done"), sem("wo_done"), sem("attn_done")
        up_done, gelu_done, hi_done, lo_done = sem("up_done"), sem("gelu_done"), sem("hi_done"), sem("lo_done")
        down_done, added = sem("down_done"), sem("added")
        sil_done, fin1_done, fin2_done, out_done = sem("sil_done"), sem("fin1_done"), sem("fin2_done"), sem("out_done")

        def wait(eng, s, value):
            if not isinstance(value, int) or value > 0:
                eng.wait_ge(s, value)

        def phases(eng, phase, tail):
            def blk(pair, k):
                return (2 * pair + k, pair + k // 2, k % 2)

            phase(None, blk(0, 0), True)
            phase(blk(0, 0), blk(0, 1), True)
            phase(blk(0, 1), blk(1, 0), True)
            phase(blk(1, 0), blk(1, 1), True)
            with eng.Fori(1, blocks // 2 - 1) as pair:
                phase(blk(pair, 1), blk(pair, 2), True)
                phase(blk(pair, 2), blk(pair, 3), True)
            last = blk(0, blocks - 1)
            phase(last, blk(0, blocks), False)
            tail(last)

        block = ctx.enter_context(nc.Block())

        @block.sync
        def _(sp):
            sp.dma_start(x_in[0][:, :, :], xb[0]).then_inc(x_loaded[0], 16)
            for dst, src in ((wall[:, CQ:CQ + KW], Wq), (wall[:, CK:CK + KW], Wk), (wall[:, CV:CV + P], Wv),
                             (wall[:, CO:CO + P], Wg), (wg1_in[:, :], Wg1), (wg2_in[:, :], Wg2),
                             (router_in[:, :], router_w), (wo[:, :], Wo),
                             (bg_row[:, :], bg.rearrange("(a n) -> a n", a=1))):
                sp.dma_start(dst, src).then_inc(w_small, 16)
            sp.dma_start(w1_raw[:, :, :], w1.rearrange("e d f -> d e f")).then_inc(w_moe, 16)
            sp.dma_start(w2_raw[:, :, :, :], w2.rearrange("e (h p) d -> p e h d", p=P)).then_inc(w_moe, 16)

            def phase(cur, nxt, more):
                n, half, par = nxt
                if more:
                    if not (isinstance(n, int) and n == 0):
                        wait(sp, xn_done, 1 * (n - 1))
                        sp.dma_start(x_in[par][:, :, :], xb[n]).then_inc(x_loaded[par], 16)
                if cur is not None:
                    b, bh, bp = cur
                    wait(sp, out_done, b - 1)
                    sp.dma_start(x_res[bp][:, :, :], xb[b]).then_inc(res_loaded[bp], 16)
                    store((n - 2, half - 1, par))

            def store(blk):
                b, bh, bp = blk
                if isinstance(b, int) and b < 0:
                    return
                wait(sp, out_done, b + 1)
                sp.dma_start(ob[b], y_out[bp][:, :, :]).then_inc(stored[bp], 16)

            def tail(blk):
                store(blk)
                sp.wait_ge(stored[0], 16 * (blocks // 2))
                sp.wait_ge(stored[1], 16 * (blocks // 2))

            phases(sp, phase, tail)

        @block.gpsimd
        def _(pool):
            pool.memset(ones_row[:, :], 1.0).then_inc(ones_made, 1)
            made = 0
            for m, v in ((ident, 0.0), (tri, 1.0), (first_half, 1.0), (second_half, 1.0), (last_row, 1.0),
                         (carry[0], 0.0), (carry[1], 0.0), (minus_half, -0.5)):
                pool.memset(m[:, :], v).then_inc(consts, 1)
                made += 1
            for e in range(EXPERTS):
                pool.memset(expert_no[:, :, e:e + 1], float(e)).then_inc(consts, 1)
                made += 1
            pool.wait_ge(consts, made)
            for m, op, base, rows, cols, fill in (
                    (ident, ALU.not_equal, 0, 1, -1, 1.0),
                    (tri, ALU.is_ge, 0, -1, 1, 0.0),
                    (first_half, ALU.is_ge, P // 2 - 1, -1, 0, 0.0),
                    (second_half, ALU.is_ge, -(P // 2), 1, 0, 0.0),
                    (last_row, ALU.is_ge, 1 - P, 1, 0, 0.0)):
                pool.affine_select(out=m[:, :], in_=m[:, :], compare_op=op, fill=fill, base=base,
                                   pattern=[[cols, P]], channel_multiplier=rows).then_inc(consts, 1)

            def hi(b, bp, e):
                for f in range(FH):
                    h = 2 * e + f
                    wait(pool, gelu_done, 16 * b + h + 1)
                    wait(pool, down_done, 8 * b + e - 1)
                    pool.sem_inc(pool_past, 1)
                    pool.tensor_copy(h_hi[h % 4][:, :], h_act[f][:, :]).then_inc(hi_done, 1)

            def outer(b, bp, j):
                wait(pool, qk_done, 2 * b + 2)
                wait(pool, state_done, 4 * (b - 1) + 4)
                kk = k_dec[bp][:, j, :].rearrange("p (h k a) -> p h k a", h=HEADS, a=1).broadcast_to([P, HEADS, DK, DV])
                vv = proj[bp][:, j, CV:CV + P].rearrange("p (h a v) -> p h a v", h=HEADS, a=1).broadcast_to([P, HEADS, DK, DV])
                pool.tensor_tensor(kv[j][:, :].rearrange("p (h k v) -> p h k v", h=HEADS, k=DK), kk, vv,
                                   ALU.mult).then_inc(kv_done, 1)

            def phase(cur, nxt, more):
                n, half, par = nxt
                for e in range(EXPERTS):
                    if cur is not None:
                        b, bh, bp = cur
                        if e == 0:
                            outer(b, bp, 0)
                            outer(b, bp, 2)
                        if e == 1:
                            outer(b, bp, 1)
                            outer(b, bp, 3)
                            wait(pool, gate_done, b)
                            pool.tensor_tensor(gate_in[:, :, :], proj[bp][:, :, CO:CO + P],
                                               bias[:, :].rearrange("p (a n) -> p a n", a=1).broadcast_to([P, TILES, P]),
                                               ALU.add).then_inc(gate_in_done, 1)
                        hi(b, bp, e)
                    if more and e == 0:
                        wait(pool, ln_step, 3 * n + 3)
                        wait(pool, xn_done, n)
                        pool.tensor_tensor(rstd[:, :], var_eps[:, :], minus_half[:, 0:TILES],
                                           ALU.pow).then_inc(rstd_done, 1)
                    if more and e == 6:
                        wait(pool, e_done, 3 * n + 3)
                        wait(pool, qs_done, 4 * (n - 1))
                        wait(pool, kv_done, 4 * (n - 1))
                        pool.tensor_tensor(q_dec[par][:, :, :], proj[par][:, :, CQ:CQ + KW], e_pos[:, :, :],
                                           ALU.mult).then_inc(qk_done, 1)
                        pool.tensor_tensor(k_dec[par][:, :, :], proj[par][:, :, CK:CK + KW], e_neg[:, :, :],
                                           ALU.mult).then_inc(qk_done, 1)
                    if cur is not None and e == 5:
                        wait(pool, o_ve_done, b + 1)
                        wait(pool, o_n_done, b)
                        pool.tensor_tensor(o_r[:, :], o_ve[:, :], minus_half[:, :], ALU.pow).then_inc(o_r_done, 1)

            phases(pool, phase, lambda blk: None)

        @block.scalar
        def _(act):
            def gelu(b, e):
                for f in range(FH):
                    h = 2 * e + f
                    wait(act, up_done, 16 * b + h + 1)
                    wait(act, lo_done, 16 * b + h - 1)
                    act.activation(h_act[f][:, :], h_ps[f][:, :], ACT.Gelu).then_inc(gelu_done, 1)

            def silu_tanh(b, bp):
                wait(act, added, 8 * b + 8)
                wait(act, fin2_done, b)
                act.activation(sil_t[:, :], acc[bp][:, :, :].rearrange("p t d -> p (t d)"), ACT.Tanh,
                               scale=0.5).then_inc(sil_done, 1)

            def phase(cur, nxt, more):
                n, half, par = nxt
                for e in range(EXPERTS):
                    if cur is not None:
                        b, bh, bp = cur
                        gelu(b, e)
                        if e == 1 and not (isinstance(b, int) and b == 0):
                            silu_tanh(b - 1, 1 - bp)
                        if e == 2:
                            wait(act, gate_in_done, b + 1)
                            wait(act, gate_done, b)
                            act.activation(gate_t[:, :, :], gate_in[:, :, :], ACT.Tanh, scale=0.5).then_inc(gate_t_done, 1)
                        if e == 4:
                            wait(act, o_done, 4 * b + 4)
                            wait(act, o_var_done, b)
                            act.activation(o_sq[:, :, :], o[:, :, :], ACT.Square).then_inc(o_sq_done, 1)
                        if e == 6:
                            wait(act, go_turned, b + 1)
                            wait(act, wo_done, b)
                            act.activation(go_t[:, :], turn_ps[:, :], ACT.Copy).then_inc(go_t_done, 1)
                        if e == 7:
                            wait(act, wo_done, b + 1)
                            wait(act, fin1_done, b - 1)
                            act.activation(attn[bp][:, :], turn_ps[:, :], ACT.Copy).then_inc(attn_done, 1)
                    if more and e == 1:
                        wait(act, xt_turned, n + 1)
                        wait(act, up_done, 16 * (n - 1))
                        wait(act, proj_done, 4 * (n - 1))
                        act.activation(xt_hi[par][:, :], turn_ps[:, :], ACT.Copy).then_inc(xt_hi_done, 1)
                    if more and e in (2, 3):
                        for j in (2 * e - 4, 2 * e - 3):
                            wait(act, proj_done, 4 * n + j + 1)
                            if j == 0:
                                wait(act, kv_done, 4 * (n - 1))
                                wait(act, gate_in_done, n - 1)
                                wait(act, mix_done, n - 1)
                                wait(act, qk_done, 2 * (n - 1))
                                wait(act, log_g_done, n - 1)
                            act.activation(proj[par][:, j, :], proj_ps[:, 0:CW], ACT.Copy).then_inc(proj_copied, 1)
                    if more and e == 4:
                        wait(act, gap_done, n + 1)
                        wait(act, router_step, 5 * n - 1)
                        act.activation(gap_t[:, :], gap[:, :], ACT.Tanh, scale=0.5).then_inc(gap_t_done, 1)
                        wait(act, kg_neg_done, n + 1)
                        wait(act, kg_ln_done, n)
                        act.activation(kg_exp[:, :, :], kg_neg[:, :, :], ACT.Exp).then_inc(kg_exp_done, 1)
                        wait(act, kg_exp_done, n + 1)
                        wait(act, log_g_done, n)
                        act.activation(kg_ln[:, :, :], kg_exp[:, :, :], ACT.Ln, bias=1.0).then_inc(kg_ln_done, 1)
                    if more and e == 6:
                        wait(act, decay_done, n + 1)
                        wait(act, qk_done, 2 * n)
                        wait(act, carry_done, 2 * (n - 1))
                        dec = proj_ps[:, 0:TILES * KW].rearrange("p (t k) -> p t k", t=TILES)
                        act.activation(e_pos[:, :, :], dec, ACT.Exp, scale=1.0 / GATE_NORM).then_inc(e_done, 1)
                        act.activation(e_neg[:, :, :], dec, ACT.Exp, scale=-1.0 / GATE_NORM).then_inc(e_done, 1)
                        act.activation(carry_dec[par][:, :, :],
                                       proj_ps[:, TILES * KW:(TILES + 2) * KW].rearrange("p (s k) -> p s k", s=2),
                                       ACT.Exp, scale=1.0 / GATE_NORM).then_inc(e_done, 1)

            phases(act, phase, lambda blk: silu_tanh(blk[0], blk[2]))

        @block.vector
        def _(dve):
            dve.wait_ge(w_small, 16 * 9)
            dve.tensor_reduce(vmean[:, :], wall[:, CV:CV + P].rearrange("p (h v) -> p h v", v=DV), AX_X,
                              ALU.add).then_inc(wprep, 1)
            dve.tensor_scalar(wall[:, CK:CK + KW], wall[:, CK:CK + KW], DK ** -0.5, None, ALU.mult).then_inc(wprep, 1)
            dve.wait_ge(wprep_pe, 1)
            dve.tensor_copy(wg1_t[:, :], turn_ps[0:16, 0:P]).then_inc(wprep, 1)
            dve.tensor_copy(wall[:, CR:CR + EXPERTS], turn_ps[:, P:P + EXPERTS]).then_inc(wprep, 1)
            dve.tensor_copy(bias[:, :], turn_ps[:, 2 * P:3 * P]).then_inc(wprep, 1)
            dve.wait_ge(wprep, 5)
            vv = wall[:, CV:CV + P].rearrange("p (h v) -> p h v", v=DV)
            dve.scalar_tensor_tensor(out=vv, in0=vmean[:, :].rearrange("p (h a) -> p h a", a=1).broadcast_to([P, HEADS, DV]),
                                     scalar=-1.0 / DV, in1=vv, op0=ALU.mult, op1=ALU.add).then_inc(wprep, 1)
            dve.wait_ge(wprep_pe, 2)
            dve.tensor_copy(wall[:, CG:CG + KW], proj_ps[:, 0:KW]).then_inc(wprep, 1)
            dve.wait_ge(consts, 16 + 5)
            dve.tensor_tensor(decay_sum[:, :], tri[:, :], first_half[:, :], ALU.subtract).then_inc(wprep, 1)
            dve.wait_ge(wprep, 8)
            dve.tensor_copy(wall_hi[:, :], wall[:, :]).then_inc(wprep, 1)
            dve.wait_ge(wprep, 9)
            dve.tensor_tensor(wall_lo[:, :], wall[:, :], wall_hi[:, :], ALU.subtract).then_inc(split_done, 1)
            def split_moe():
                dve.wait_ge(w_moe, 32)
                dve.tensor_copy(w1_hi[:, :, :], w1_raw[:, :, :]).then_inc(wprep, 1)
                dve.tensor_copy(w2_hi[:, :, :, :], w2_raw[:, :, :, :]).then_inc(wprep, 1)
                dve.wait_ge(wprep, 11)
                dve.tensor_tensor(w1_lo[:, :, :], w1_raw[:, :, :], w1_hi[:, :, :], ALU.subtract).then_inc(split_done, 1)
                dve.tensor_tensor(w2_lo[:, :, :, :], w2_raw[:, :, :, :], w2_hi[:, :, :, :],
                                  ALU.subtract).then_inc(split_done, 1)

            def layer_norm(n, half, par):
                wait(dve, x_loaded[par], 16 * (half + 1))
                wait(dve, ln_step, 3 * n - 1)
                wait(dve, xn_done, n)
                wait(dve, rstd_done, n)
                for j in range(TILES):
                    i = dve.bn_stats(stats[:, j, :], x_in[par][:, j, :])
                i.then_inc(ln_step, 1)
                wait(dve, ln_step, 3 * n + 1)
                dve.sem_inc(dve_past, 1)
                for j in range(TILES):
                    i = dve.bn_aggr(moments[:, j, :], stats[:, j, :])
                i.then_inc(ln_step, 1)
                wait(dve, ln_step, 3 * n + 2)
                dve.tensor_scalar(var_eps[:, :], moments[:, :, 1], EPS, None, ALU.add).then_inc(ln_step, 1)

            def normalise(n, half, par):
                wait(dve, rstd_done, n + 1)
                wait(dve, xt_turned, n)
                for j in range(TILES):
                    i = dve.tensor_scalar(xn[:, j, :], x_in[par][:, j, :], moments[:, j, 0:1], rstd[:, j:j + 1],
                                          ALU.subtract, ALU.mult)
                i.then_inc(xn_done, 1)

            def x_low(n, par):
                wait(dve, xt_hi_done, n + 1)
                dve.tensor_tensor(xt_lo[par][:, :], turn_ps[:, :], xt_hi[par][:, :], ALU.subtract).then_inc(xt_lo_done, 1)

            def router(n, par):
                wait(dve, proj_copied, 4 * n + 4)
                wait(dve, kg_exp_done, n)
                wait(dve, mix_done, n)
                wait(dve, gap_t_done, n)
                kg = proj[par][:, :, CG:CG + KW]
                dve.scalar_tensor_tensor(out=kg_neg[:, :, :], in0=kg, scalar=-1.0, in1=kg, op0=ALU.mult,
                                         op1=ALU.min).then_inc(kg_neg_done, 1)
                for j in range(TILES):
                    i = dve.max(top[:, j, :], proj[par][:, j, CR:CR + EXPERTS])
                i.then_inc(router_step, 1)
                wait(dve, router_step, 5 * n + 1)
                dve.tensor_tensor(gap[:, :], top[:, :, 1], top[:, :, 0], ALU.subtract).then_inc(gap_done, 1)
                for j in range(TILES):
                    i = dve.max_index(top_no[:, j, :], top[:, j, :], proj[par][:, j, CR:CR + EXPERTS])
                i.then_inc(router_step, 1)
                wait(dve, router_step, 5 * n + 2)
                dve.tensor_copy(top_nof[:, :, :], top_no[:, :, :]).then_inc(router_step, 1)
                wait(dve, router_step, 5 * n + 3)
                for k, pick in enumerate((pick1, pick2)):
                    i = dve.tensor_tensor(pick[:, :, :], expert_no[:, :, :],
                                          top_nof[:, :, k:k + 1].broadcast_to([P, TILES, EXPERTS]), ALU.is_equal)
                wait(dve, gap_t_done, n + 1)
                dve.tensor_scalar(p1[:, :], gap_t[:, :], -0.5, 0.5, ALU.mult, ALU.add)
                dve.tensor_scalar(p2[:, :], gap_t[:, :], 0.5, 0.5, ALU.mult, ALU.add).then_inc(router_step, 1)
                wait(dve, router_step, 5 * n + 4)
                for pick, pk in ((pick1, p1), (pick2, p2)):
                    i = dve.tensor_tensor(pick[:, :, :], pick[:, :, :],
                                          pk[:, :].rearrange("p (t a) -> p t a", a=1).broadcast_to([P, TILES, EXPERTS]), ALU.mult)
                i.then_inc(router_step, 1)
                wait(dve, router_step, 5 * n + 5)
                wait(dve, added, 8 * (n - 1))
                dve.tensor_tensor(mix[par][:, :, :], pick1[:, :, :], pick2[:, :, :], ALU.add).then_inc(mix_done, 1)

            def log_gate(n, par):
                wait(dve, kg_ln_done, n + 1)
                wait(dve, decay_done, n)
                dve.scalar_tensor_tensor(out=log_g[:, :, :], in0=proj[par][:, :, CG:CG + KW], scalar=0.0,
                                         in1=kg_ln[:, :, :], op0=ALU.min, op1=ALU.subtract).then_inc(log_g_done, 1)

            ORDER = (0, 2, 1, 3)

            def carry_on(b, bp, s):
                wait(dve, state_done, 4 * b + s + 1)
                wait(dve, state_done, 4 * (b - 1) + 4)
                dd = carry_dec[bp][96:P, s, :].rearrange("p (h k a) -> p h k a", h=HEADS, a=1).broadcast_to([P - 96, HEADS, DK, DV])
                dve.tensor_tensor(carry[s][96:P, :].rearrange("p (h k v) -> p h k v", h=HEADS, k=DK),
                                  state_ps[s][96:P, :].rearrange("p (h k v) -> p h k v", h=HEADS, k=DK), dd,
                                  ALU.mult).then_inc(carry_done, 1)

            def read_state(b, bp, i):
                j = ORDER[i]
                wait(dve, o_done, 4 * b + i - 1)
                wait(dve, state_done, 4 * b + i + 1)
                qq = q_dec[bp][:, j, :].rearrange("p (h k a) -> p h k a", h=HEADS, a=1).broadcast_to([P, HEADS, DK, DV])
                dve.tensor_tensor(qs[i % 2][:, :].rearrange("p (h k v) -> p h k v", h=HEADS, k=DK),
                                  state_ps[j // 2][:, :].rearrange("p (h k v) -> p h k v", h=HEADS, k=DK), qq,
                                  ALU.mult).then_inc(qs_done, 1)

            def sum_keys(b, bp, i):
                j = ORDER[i]
                wait(dve, qs_done, 4 * b + i + 1)
                if i == 0:
                    wait(dve, o_n_done, b)
                dve.tensor_reduce(o[:, j, :].rearrange("p (h v) -> p h v", h=HEADS),
                                  qs[i % 2][:, :].rearrange("p (h k v) -> p h v k", h=HEADS, k=DK), AX_X,
                                  ALU.add).then_inc(o_done, 1)

            def head_var(b):
                wait(dve, o_sq_done, b + 1)
                wait(dve, o_r_done, b)
                dve.tensor_reduce(o_var[:, :], o_sq[:, :, :].rearrange("p t (h v) -> p (t h) v", v=DV), AX_X,
                                  ALU.add).then_inc(o_var_done, 1)
                wait(dve, o_var_done, b + 1)
                dve.tensor_scalar(o_ve[:, :], o_var[:, :], 4.0 / DV, 4.0 * EPS, ALU.mult,
                                  ALU.add).then_inc(o_ve_done, 1)

            def gate_silu(b):
                wait(dve, gate_t_done, b + 1)
                wait(dve, go_done, b)
                dve.scalar_tensor_tensor(out=gate[:, :, :], in0=gate_t[:, :, :], scalar=1.0, in1=gate_in[:, :, :],
                                         op0=ALU.add, op1=ALU.mult).then_inc(gate_done, 1)

            def gated(b):
                wait(dve, o_r_done, b + 1)
                wait(dve, go_done, b)
                dve.tensor_tensor(o_n[:, :, :].rearrange("p t (h v) -> p (t h) v", v=DV),
                                  o[:, :, :].rearrange("p t (h v) -> p (t h) v", v=DV),
                                  o_r[:, :].rearrange("p (h a) -> p h a", a=1).broadcast_to([P, TILES * HEADS, DV]),
                                  ALU.mult).then_inc(o_n_done, 1)
                wait(dve, o_n_done, b + 1)
                wait(dve, gate_done, b + 1)
                wait(dve, go_turned, b)
                dve.tensor_tensor(go[:, :, :], o_n[:, :, :], gate[:, :, :], ALU.mult).then_inc(go_done, 1)

            def low(b, e):
                for f in range(FH):
                    h = 2 * e + f
                    wait(dve, hi_done, 16 * b + h + 1)
                    wait(dve, down_done, 8 * b + e - 1)
                    dve.tensor_tensor(h_lo[h % 4][:, :], h_act[f][:, :], h_hi[h % 4][:, :],
                                      ALU.subtract).then_inc(lo_done, 1)

            def add_expert(b, bp, e):
                wait(dve, down_done, 8 * b + e + 1)
                if e == 0:
                    wait(dve, mix_done, b + 1)
                    wait(dve, fin1_done, b - 1)
                else:
                    wait(dve, added, 8 * b + e)
                for j in range(TILES):
                    y, w = y_ps[e % 2][:, j * P:(j + 1) * P], mix[bp][:, j, e:e + 1]
                    if e == 0:
                        i = dve.tensor_scalar(acc[bp][:, j, :], y, w, None, ALU.mult)
                    else:
                        i = dve.scalar_tensor_tensor(out=acc[bp][:, j, :], in0=y, scalar=w, in1=acc[bp][:, j, :],
                                                     op0=ALU.mult, op1=ALU.add)
                i.then_inc(added, 1)

            def finish(b, bh, bp):
                wait(dve, attn_done, b + 1)
                wait(dve, out_done, b)
                wait(dve, added, 8 * b + 8)
                dve.tensor_tensor(fin1[:, :], acc[bp][:, :, :].rearrange("p t d -> p (t d)"), attn[bp][:, :],
                                  ALU.mult).then_inc(fin1_done, 1)
                wait(dve, fin1_done, b + 1)
                wait(dve, sil_done, b + 1)
                dve.scalar_tensor_tensor(out=fin2[:, :], in0=sil_t[:, :], scalar=1.0, in1=fin1[:, :], op0=ALU.add,
                                         op1=ALU.mult).then_inc(fin2_done, 1)
                wait(dve, fin2_done, b + 1)
                wait(dve, res_loaded[bp], 16 * (bh + 1))
                wait(dve, stored[bp], 16 * bh)
                dve.scalar_tensor_tensor(out=y_out[bp][:, :, :].rearrange("p t d -> p (t d)"), in0=fin2[:, :],
                                         scalar=0.5, in1=x_res[bp][:, :, :].rearrange("p t d -> p (t d)"),
                                         op0=ALU.mult, op1=ALU.add).then_inc(out_done, 1)

            def phase(cur, nxt, more):
                n, half, par = nxt
                for e in range(EXPERTS):
                    if more and e == 0:
                        layer_norm(n, half, par)
                    if cur is not None:
                        b, bh, bp = cur
                        first = isinstance(b, int) and b == 0
                        low(b, e)
                        if e:
                            add_expert(b, bp, e - 1)
                        elif not first:
                            add_expert(b - 1, 1 - bp, EXPERTS - 1)
                        if e == 1:
                            carry_on(b, bp, 0)
                            carry_on(b, bp, 1)
                            read_state(b, bp, 0)
                            read_state(b, bp, 1)
                        if e == 2:
                            sum_keys(b, bp, 0)
                            sum_keys(b, bp, 1)
                            if not first:
                                finish(b - 1, bh - 1 + bp, 1 - bp)
                        if e == 3:
                            read_state(b, bp, 2)
                            read_state(b, bp, 3)
                            sum_keys(b, bp, 2)
                            sum_keys(b, bp, 3)
                        if e == 4:
                            gate_silu(b)
                        if e == 5:
                            head_var(b)
                        if e == 6:
                            gated(b)
                    elif e == 4:
                        split_moe()
                    if more and e == 0:
                        normalise(n, half, par)
                    if more and e == 1:
                        x_low(n, par)
                    if more and e == 4:
                        router(n, par)
                    if more and e == 5:
                        log_gate(n, par)

            def tail(blk):
                b, bh, bp = blk
                add_expert(b, bp, EXPERTS - 1)
                finish(b, bh, bp)

            phases(dve, phase, tail)

        @block.tensor
        def _(pe):
            pe.wait_ge(consts, 16 + 5)
            pe.wait_ge(ones_made, 1)
            pe.wait_ge(w_small, 16 * 9)
            pe.transpose(turn_ps[0:16, 0:P], wg1_in[:, :], ident[:, :])
            pe.transpose(turn_ps[:, P:P + EXPERTS], router_in[:, :], ident[0:EXPERTS, 0:EXPERTS])
            pe.matmul(turn_ps[:, 2 * P:3 * P], ones_row[:, :], bg_row[:, :], start=True, stop=True).then_inc(wprep_pe, 1)
            pe.wait_ge(wprep, 5)
            pe.matmul(proj_ps[:, 0:KW], wg1_t[:, :], wg2_in[:, :], start=True, stop=True).then_inc(wprep_pe, 1)
            pe.wait_ge(split_done, 1)

            def three(dst, a_hi, a_lo, b_hi, b_lo, start=True, stop=True):
                pe.matmul(dst, a_hi, b_hi, start=start, stop=False)
                pe.matmul(dst, a_hi, b_lo, start=False, stop=False)
                return pe.matmul(dst, a_lo, b_hi, start=False, stop=stop)

            def up(b, bp, e):
                if e == 0:
                    wait(pe, xt_lo_done, b + 1)
                    if isinstance(b, int) and b == 0:
                        pe.wait_ge(split_done, 3)
                for f in range(FH):
                    h = 2 * e + f
                    wait(pe, gelu_done, 16 * b + h - 1)
                    c = slice(f * P, (f + 1) * P)
                    three(h_ps[f][:, :], w1_hi[:, e, c], w1_lo[:, e, c], xt_hi[bp][:, :],
                          xt_lo[bp][:, :]).then_inc(up_done, 1)

            def down(b, e):
                wait(pe, lo_done, 16 * b + 2 * e + 2)
                wait(pe, added, 8 * b + e - 1)
                for j in range(TILES):
                    c = slice(j * P, (j + 1) * P)
                    for f in range(FH):
                        h = (2 * e + f) % 4
                        i = three(y_ps[e % 2][:, c], h_hi[h][:, c], h_lo[h][:, c], w2_hi[:, e, f, :],
                                  w2_lo[:, e, f, :], start=(f == 0), stop=(f == FH - 1))
                i.then_inc(down_done, 1)

            def project(n, par, j):
                if j == 0:
                    wait(pe, xt_lo_done, n + 1)
                    wait(pe, e_done, 3 * n)
                else:
                    wait(pe, proj_copied, 4 * n + j)
                c = slice(j * P, (j + 1) * P)
                three(proj_ps[:, 0:CW], xt_hi[par][:, c], xt_lo[par][:, c], wall_hi[:, :],
                      wall_lo[:, :]).then_inc(proj_done, 1)

            def states(b, i, j):
                wait(pe, kv_done, 4 * b + i + 1)
                s = j // 2
                if i < 2:
                    wait(pe, qs_done, 4 * (b - 1) + i + 3)
                    pe.matmul(state_ps[s][:, :], tri[:, :], kv[j][:, :], start=True, stop=True).then_inc(state_done, 1)
                else:
                    wait(pe, qs_done, 4 * b + i - 1)
                    wait(pe, carry_done, 2 * b + s + 1)
                    pe.matmul(state_ps[s][:, :], tri[:, :], kv[j][:, :], start=True, stop=False)
                    pe.matmul(state_ps[s][:, :], last_row[:, :], carry[s][:, :], start=False,
                              stop=True).then_inc(state_done, 1)

            def phase(cur, nxt, more):
                n, half, par = nxt
                for e in range(EXPERTS):
                    if cur is not None:
                        b, bh, bp = cur
                        up(b, bp, e)
                        if e == 1:
                            states(b, 0, 0)
                            states(b, 1, 2)
                        if e == 2:
                            states(b, 2, 1)
                            states(b, 3, 3)
                        if e == 7:
                            wait(pe, go_t_done, b + 1)
                            for j in range(TILES):
                                c = slice(j * P, (j + 1) * P)
                                i = pe.matmul(turn_ps[:, c], go_t[:, c], wo[:, :], start=True, stop=True)
                            i.then_inc(wo_done, 1)
                    if more and e == 1:
                        wait(pe, xn_done, n + 1)
                        wait(pe, attn_done, n - 1)
                        for j in range(TILES):
                            i = pe.transpose(turn_ps[:, j * P:(j + 1) * P], xn[:, j, :], ident[:, :])
                        i.then_inc(xt_turned, 1)
                    if more and e in (2, 3):
                        project(n, par, 2 * e - 4)
                        project(n, par, 2 * e - 3)
                    if more and e == 6:
                        wait(pe, log_g_done, n + 1)
                        wait(pe, proj_copied, 4 * n + 4)
                        pe.matmul(proj_ps[:, 0:TILES * KW], decay_sum[:, :],
                                  log_g[:, :, :].rearrange("p t k -> p (t k)"), start=True, stop=True)
                        dst = proj_ps[:, TILES * KW:(TILES + 2) * KW].rearrange("p (s k) -> p s k", s=2)
                        pe.matmul(dst, second_half[:, :], log_g[:, 0:TILES:2, :], start=True, stop=False)
                        pe.matmul(dst, first_half[:, :], log_g[:, 1:TILES:2, :], start=False,
                                  stop=True).then_inc(decay_done, 1)
                    if cur is not None:
                        if e:
                            down(b, e - 1)
                        elif not (isinstance(b, int) and b == 0):
                            down(b - 1, EXPERTS - 1)
                        if e == 6:
                            wait(pe, go_done, b + 1)
                            wait(pe, xt_lo_done, b + (2 if more else 1))
                            for j in range(TILES):
                                i = pe.transpose(turn_ps[:, j * P:(j + 1) * P], go[:, j, :], ident[:, :])
                            i.then_inc(go_turned, 1)

            phases(pe, phase, lambda blk: down(blk[0], EXPERTS - 1))


_INS = ['L0_attn_inputs', 'L0_attn_Wq', 'L0_attn_Wk', 'L0_attn_Wg1', 'L0_attn_Wg2', 'L0_attn_Wv', 'L0_attn_Wg',
        'L0_attn_bg', 'L0_attn_Wo', 'L0_ffn_router_w', 'L0_ffn_w1', 'L0_ffn_w2']
_OUTS = [((32, 256, 128), 'float32')]


def kernel(**inputs):
    import numpy as _np
    import concourse.bacc as _bacc
    from concourse import mybir as _mybir
    from concourse.bass_utils import run_bass_kernel_spmd as _run

    nc = _bacc.Bacc("TRN2", target_bir_lowering=False, num_devices=1)
    arrays, args = {}, []
    for name in _INS:
        a = _np.ascontiguousarray(inputs[name])
        arrays[f"in_{name}_dram"] = a
        args.append(nc.dram_tensor(f"in_{name}_dram", a.shape, _mybir.dt.from_np(a.dtype), kind="ExternalInput").ap())
    for i, (shape, dtype) in enumerate(_OUTS):
        dt = _mybir.dt.from_np(_np.dtype(dtype))
        args.append(nc.dram_tensor(f"out_{i}_dram", shape, dt, kind="ExternalOutput").ap())
    gla_moe_kernel(nc, *args)
    r = _run(nc, [arrays], core_ids=[0])
    got = tuple(r.results[0][f"out_{i}_dram"] for i in range(len(_OUTS)))
    return got[0]
```

```python
from contextlib import ExitStack

import concourse.bass as bass
from concourse import mybir

ALU = mybir.AluOpType
ACT = mybir.ActivationFunctionType
AX_X = mybir.AxisListType.X
F32 = mybir.dt.float32
F16 = mybir.dt.float16
U32 = mybir.dt.uint32

P = 128
TILES = 4
TOK = TILES * P
HEADS, DK, DV = 16, 4, 8
KW = HEADS * DK
SW = HEADS * DK * DV
EXPERTS = 8
FH = 2
GATE_NORM = 16.0
EPS = 1e-5
CQ, CK, CG, CR, CV, CO, CW = 0, 64, 128, 192, 200, 328, 456


def gla_moe_kernel(nc, x, Wq, Wk, Wg1, Wg2, Wv, Wg, bg, Wo, router_w, w1, w2, out):
    blocks = x.shape[0] * x.shape[1] // TOK
    assert blocks % 2 == 0 and blocks >= 6
    xb = x.rearrange("(n s) (c p) d -> n p (s c) d", s=2, p=P)
    ob = out.rearrange("(n s) (c p) d -> n p (s c) d", s=2, p=P)

    with ExitStack() as ctx:
        def sb(name, shape, dt=F32):
            return ctx.enter_context(nc.sbuf_tensor(name, shape, dt))

        def sem(name):
            return ctx.enter_context(nc.semaphore(name))

        def ps(name):
            return ctx.enter_context(nc.psum_tensor(name, [P, 512], F32))

        h_ps = [ps(f"h_ps{i}") for i in range(2)]
        y_ps = [ps(f"y_ps{i}") for i in range(2)]
        proj_ps = ps("proj_ps")
        state_ps = [ps(f"state_ps{i}") for i in range(2)]
        turn_ps = ps("turn_ps")

        wall = sb("wall", [P, CW])
        wall_hi, wall_lo = sb("wall_hi", [P, CW], F16), sb("wall_lo", [P, CW], F16)
        w1_raw, w2_raw = sb("w1_raw", [P, EXPERTS, 256]), sb("w2_raw", [P, EXPERTS, FH, P])
        w1_hi, w1_lo = sb("w1_hi", [P, EXPERTS, 256], F16), sb("w1_lo", [P, EXPERTS, 256], F16)
        w2_hi, w2_lo = sb("w2_hi", [P, EXPERTS, FH, P], F16), sb("w2_lo", [P, EXPERTS, FH, P], F16)
        wo = sb("wo", [P, P])
        wg1_in, wg2_in, router_in = sb("wg1_in", [P, 16]), sb("wg2_in", [16, KW]), sb("router_in", [EXPERTS, P])
        wg1_t = sb("wg1_t", [16, P])
        vmean = sb("vmean", [P, HEADS])
        bg_row, ones_row, bias = sb("bg_row", [1, P]), sb("ones_row", [1, P]), sb("bias", [P, P])
        ident, tri, first_half = sb("ident", [P, P]), sb("tri", [P, P]), sb("first_half", [P, P])
        second_half, last_row, decay_sum = sb("second_half", [P, P]), sb("last_row", [P, P]), sb("decay_sum", [P, P])
        expert_no = sb("expert_no", [P, TILES, EXPERTS])
        minus_half = sb("minus_half", [P, TILES * HEADS])

        x_in = [sb(f"x_in{i}", [P, TILES, P]) for i in range(2)]
        x_res = [sb(f"x_res{i}", [P, TILES, P]) for i in range(2)]
        y_out = [sb(f"y_out{i}", [P, TILES, P]) for i in range(2)]
        acc = [sb(f"acc{i}", [P, TILES, P]) for i in range(2)]
        attn = [sb(f"attn{i}", [P, TOK]) for i in range(2)]
        xt_hi = [sb(f"xt_hi{i}", [P, TOK], F16) for i in range(2)]
        xt_lo = [sb(f"xt_lo{i}", [P, TOK], F16) for i in range(2)]
        proj = [sb(f"proj{i}", [P, TILES, CW]) for i in range(2)]
        q_dec, k_dec, carry_dec = sb("q_dec", [P, TILES, KW]), sb("k_dec", [P, TILES, KW]), sb("carry_dec", [P, 2, KW])
        mix = [sb(f"mix{i}", [P, TILES, EXPERTS]) for i in range(2)]
        stats, moments = sb("stats", [P, TILES, 6]), sb("moments", [P, TILES, 2])
        var_eps, rstd = sb("var_eps", [P, TILES]), sb("rstd", [P, TILES])
        xn = sb("xn", [P, TILES, P])
        kg_neg, kg_exp, kg_ln, log_g = (sb(n, [P, TILES, KW]) for n in ("kg_neg", "kg_exp", "kg_ln", "log_g"))
        e_pos, e_neg = sb("e_pos", [P, TILES, KW]), sb("e_neg", [P, TILES, KW])
        top, top_no = sb("top", [P, TILES, 8]), sb("top_no", [P, TILES, 8], U32)
        top_nof, gap, gap_t = sb("top_nof", [P, TILES, 8]), sb("gap", [P, TILES]), sb("gap_t", [P, TILES])
        p1, p2 = sb("p1", [P, TILES]), sb("p2", [P, TILES])
        pick1, pick2 = sb("pick1", [P, TILES, EXPERTS]), sb("pick2", [P, TILES, EXPERTS])
        kv = [sb(f"kv{i}", [P, SW]) for i in range(4)]
        carry = [sb(f"carry{i}", [P, SW]) for i in range(2)]
        qs = [sb(f"qs{i}", [P, SW]) for i in range(2)]
        o, o_sq = sb("o", [P, TILES, P]), sb("o_sq", [P, TILES, P])
        o_var, o_r = sb("o_var", [P, TILES * HEADS]), sb("o_r", [P, TILES * HEADS])
        o_ve, o_ln = sb("o_ve", [P, TILES * HEADS]), sb("o_ln", [P, TILES * HEADS])
        gate_in, gate_t, gate = (sb(n, [P, TILES, P]) for n in ("gate_in", "gate_t", "gate"))
        o_n, go = sb("o_n", [P, TILES, P]), sb("go", [P, TILES, P])
        go_t = sb("go_t", [P, TOK])
        sil_t, fin1, fin2 = (sb(n, [P, TOK]) for n in ("sil_t", "fin1", "fin2"))
        h_act = [sb(f"h_act{i}", [P, TOK]) for i in range(2)]
        h_hi = [sb(f"h_hi{i}", [P, TOK], F16) for i in range(4)]
        h_lo = [sb(f"h_lo{i}", [P, TOK], F16) for i in range(4)]

        w_small, w_moe, consts, ones_made = sem("w_small"), sem("w_moe"), sem("consts"), sem("ones_made")
        wprep, wprep_pe, split_done = sem("wprep"), sem("wprep_pe"), sem("split_done")
        dve_past = sem("dve_past")
        x_loaded = [sem(f"x_loaded{i}") for i in range(2)]
        res_loaded = [sem(f"res_loaded{i}") for i in range(2)]
        stored = [sem(f"stored{i}") for i in range(2)]
        ln_step, rstd_done, xn_done = sem("ln_step"), sem("rstd_done"), sem("xn_done")
        xt_turned, xt_hi_done, xt_lo_done = sem("xt_turned"), sem("xt_hi_done"), sem("xt_lo_done")
        proj_done, proj_copied = sem("proj_done"), sem("proj_copied")
        router_step, gap_done, gap_t_done, mix_done = sem("router_step"), sem("gap_done"), sem("gap_t_done"), sem("mix_done")
        kg_neg_done, kg_exp_done, kg_ln_done, log_g_done = (
            sem("kg_neg_done"), sem("kg_exp_done"), sem("kg_ln_done"), sem("log_g_done"))
        decay_done, e_done, q_done, k_done = sem("decay_done"), sem("e_done"), sem("q_done"), sem("k_done")
        kv_done, state_done, carry_done = sem("kv_done"), sem("state_done"), sem("carry_done")
        qs_done, o_done, o_sq_done, o_var_done, o_ve_done, o_ln_done, o_r_done = (
            sem("qs_done"), sem("o_done"), sem("o_sq_done"), sem("o_var_done"), sem("o_ve_done"), sem("o_ln_done"),
            sem("o_r_done"))
        gate_in_done, gate_t_done, gate_done, o_n_done, go_done = (
            sem("gate_in_done"), sem("gate_t_done"), sem("gate_done"), sem("o_n_done"), sem("go_done"))
        go_turned, go_t_done, wo_done, attn_done = sem("go_turned"), sem("go_t_done"), sem("wo_done"), sem("attn_done")
        up_done, gelu_done, lo_done = sem("up_done"), sem("gelu_done"), sem("lo_done")
        down_done, added = sem("down_done"), sem("added")
        sil_done, fin1_done, fin2_done, out_done = sem("sil_done"), sem("fin1_done"), sem("fin2_done"), sem("out_done")

        def wait(eng, s, value):
            if not isinstance(value, int) or value > 0:
                eng.wait_ge(s, value)

        def phases(eng, phase):
            def blk(pair, k):
                return (2 * pair + k, pair + k // 2, k % 2)
            phase(None, None, blk(0, 0))
            phase(None, blk(0, 0), blk(0, 1))
            phase(blk(0, 0), blk(0, 1), blk(0, 2))
            phase(blk(0, 1), blk(0, 2), blk(0, 3))
            with eng.Fori(1, blocks // 2 - 1) as pair:
                phase(blk(pair, 0), blk(pair, 1), blk(pair, 2))
                phase(blk(pair, 1), blk(pair, 2), blk(pair, 3))
            phase(blk(0, blocks - 2), blk(0, blocks - 1), None)
            phase(blk(0, blocks - 1), None, None)

        block = ctx.enter_context(nc.Block())

        @block.sync
        def _(sp):
            sp.dma_start(x_in[0][:, :, :], xb[0]).then_inc(x_loaded[0], 16)
            for dst, src in ((wall[:, CQ:CQ + KW], Wq), (wall[:, CK:CK + KW], Wk), (wall[:, CV:CV + P], Wv),
                             (wall[:, CO:CO + P], Wg), (wg1_in[:, :], Wg1), (wg2_in[:, :], Wg2),
                             (router_in[:, :], router_w), (wo[:, :], Wo),
                             (bg_row[:, :], bg.rearrange("(a n) -> a n", a=1))):
                sp.dma_start(dst, src).then_inc(w_small, 16)
            sp.dma_start(w1_raw[:, :, :], w1.rearrange("e d f -> d e f")).then_inc(w_moe, 16)
            sp.dma_start(w2_raw[:, :, :, :], w2.rearrange("e (h p) d -> p e h d", p=P)).then_inc(w_moe, 16)

            def phase(prv, cur, nxt):
                if nxt is not None and not (isinstance(nxt[0], int) and nxt[0] == 0):
                    n, half, par = nxt
                    wait(sp, xn_done, n - 1)
                    sp.dma_start(x_in[par][:, :, :], xb[n]).then_inc(x_loaded[par], 16)
                if cur is not None:
                    b, bh, bp = cur
                    wait(sp, out_done, b - 1)
                    sp.dma_start(x_res[bp][:, :, :], xb[b]).then_inc(res_loaded[bp], 16)
                if prv is not None:
                    store((prv[0] - 1, prv[1] - 1 + prv[2], 1 - prv[2]))

            def store(blk):
                b, bh, bp = blk
                if isinstance(b, int) and b < 0:
                    return
                wait(sp, out_done, b + 1)
                sp.dma_start(ob[b], y_out[bp][:, :, :]).then_inc(stored[bp], 16)

            phases(sp, phase)
            store((blocks - 1, blocks // 2 - 1, 1))
            sp.wait_ge(stored[0], 16 * (blocks // 2))
            sp.wait_ge(stored[1], 16 * (blocks // 2))

        @block.gpsimd
        def _(pool):
            pool.memset(ones_row[:, :], 1.0).then_inc(ones_made, 1)
            made = 0
            for m, v in ((ident, 0.0), (tri, 1.0), (first_half, 1.0), (second_half, 1.0), (last_row, 1.0),
                         (carry[0], 0.0), (carry[1], 0.0), (minus_half, -0.5)):
                pool.memset(m[:, :], v).then_inc(consts, 1)
                made += 1
            for e in range(EXPERTS):
                pool.memset(expert_no[:, :, e:e + 1], float(e)).then_inc(consts, 1)
                made += 1
            pool.wait_ge(consts, made)
            for m, op, base, rows, cols, fill in (
                    (ident, ALU.not_equal, 0, 1, -1, 1.0),
                    (tri, ALU.is_ge, 0, -1, 1, 0.0),
                    (first_half, ALU.is_ge, P // 2 - 1, -1, 0, 0.0),
                    (second_half, ALU.is_ge, -(P // 2), 1, 0, 0.0),
                    (last_row, ALU.is_ge, 1 - P, 1, 0, 0.0)):
                pool.affine_select(out=m[:, :], in_=m[:, :], compare_op=op, fill=fill, base=base,
                                   pattern=[[cols, P]], channel_multiplier=rows).then_inc(consts, 1)

            def outer(b, bp, j):
                if j == 0:
                    wait(pool, k_done, b + 1)
                    wait(pool, state_done, 4 * b)
                kk = k_dec[:, j, :].rearrange("p (h k a) -> p h k a", h=HEADS, a=1).broadcast_to([P, HEADS, DK, DV])
                vv = proj[bp][:, j, CV:CV + P].rearrange("p (h a v) -> p h a v", h=HEADS, a=1).broadcast_to([P, HEADS, DK, DV])
                pool.tensor_tensor(kv[j][:, :].rearrange("p (h k v) -> p h k v", h=HEADS, k=DK), kk, vv,
                                   ALU.mult).then_inc(kv_done, 1)

            def phase(prv, cur, nxt):
                if nxt is not None:
                    n, half, par = nxt
                    wait(pool, ln_step, 3 * n + 3)
                    wait(pool, xn_done, n)
                    pool.tensor_tensor(rstd[:, :], var_eps[:, :], minus_half[:, 0:TILES],
                                       ALU.pow).then_inc(rstd_done, 1)
                if cur is not None:
                    b, bh, bp = cur
                    wait(pool, e_done, 3 * b + 3)
                    wait(pool, qs_done, 4 * b)
                    pool.tensor_tensor(k_dec[:, :, :], proj[bp][:, :, CK:CK + KW], e_neg[:, :, :],
                                       ALU.mult).then_inc(k_done, 1)
                    outer(b, bp, 0)
                    outer(b, bp, 2)
                    pool.tensor_tensor(q_dec[:, :, :], proj[bp][:, :, CQ:CQ + KW], e_pos[:, :, :],
                                       ALU.mult).then_inc(q_done, 1)
                    outer(b, bp, 1)
                    outer(b, bp, 3)
                    wait(pool, gate_done, b)
                    pool.tensor_tensor(gate_in[:, :, :], proj[bp][:, :, CO:CO + P],
                                       bias[:, :].rearrange("p (a n) -> p a n", a=1).broadcast_to([P, TILES, P]),
                                       ALU.add).then_inc(gate_in_done, 1)

            phases(pool, phase)

        @block.scalar
        def _(act):
            def gelu(b, e):
                for f in range(FH):
                    h = 2 * e + f
                    wait(act, up_done, 16 * b + h + 1)
                    wait(act, lo_done, 16 * b + h - 1)
                    wait(act, down_done, 8 * b + e - 1)
                    act.activation(h_hi[h % 4][:, :], h_ps[f][:, :], ACT.Gelu)
                    act.activation(h_act[f][:, :], h_ps[f][:, :], ACT.Gelu).then_inc(gelu_done, 1)

            def phase(prv, cur, nxt):
                for e in range(EXPERTS):
                    if cur is not None:
                        gelu(cur[0], e)
                    if nxt is not None:
                        n, half, par = nxt
                        if e == 1:
                            wait(act, xt_turned, n + 1)
                            wait(act, up_done, 16 * (n - 1))
                            wait(act, proj_done, 4 * (n - 1))
                            act.activation(xt_hi[par][:, :], turn_ps[:, :], ACT.Copy).then_inc(xt_hi_done, 1)
                        if e in (2, 3):
                            for j in (2 * e - 4, 2 * e - 3):
                                wait(act, proj_done, 4 * n + j + 1)
                                if j == 0:
                                    wait(act, gate_in_done, n - 1)
                                    wait(act, kv_done, 4 * (n - 1))
                                    wait(act, mix_done, n - 1)
                                    wait(act, q_done, n - 1)
                                    wait(act, log_g_done, n - 1)
                                act.activation(proj[par][:, j, :], proj_ps[:, 0:CW], ACT.Copy).then_inc(proj_copied, 1)
                        if e == 4:
                            wait(act, gap_done, n + 1)
                            wait(act, router_step, 5 * n - 1)
                            act.activation(gap_t[:, :], gap[:, :], ACT.Tanh, scale=0.5).then_inc(gap_t_done, 1)
                    if e == 4:
                        act.preload_act_table_set("natural_log_exp_and_others")
                    if e == 4 and cur is not None:
                        b, bh, bp = cur
                        wait(act, decay_done, b + 1)
                        wait(act, q_done, b)
                        wait(act, carry_done, 2 * b)
                        dec = proj_ps[:, 0:TILES * KW].rearrange("p (t k) -> p t k", t=TILES)
                        act.activation(e_neg[:, :, :], dec, ACT.Exp, scale=-1.0 / GATE_NORM).then_inc(e_done, 1)
                        act.activation(e_pos[:, :, :], dec, ACT.Exp, scale=1.0 / GATE_NORM).then_inc(e_done, 1)
                        act.activation(carry_dec[:, :, :],
                                       proj_ps[:, TILES * KW:(TILES + 2) * KW].rearrange("p (s k) -> p s k", s=2),
                                       ACT.Exp, scale=1.0 / GATE_NORM).then_inc(e_done, 1)
                    if e == 4 and prv is not None:
                        m = prv[0]
                        wait(act, o_ve_done, m + 1)
                        wait(act, o_r_done, m)
                        act.activation(o_ln[:, :], o_ve[:, :], ACT.Ln).then_inc(o_ln_done, 1)
                    if e == 4 and nxt is not None:
                        wait(act, kg_neg_done, n + 1)
                        wait(act, kg_ln_done, n)
                        act.activation(kg_exp[:, :, :], kg_neg[:, :, :], ACT.Exp).then_inc(kg_exp_done, 1)
                    if e == 4 and prv is not None:
                        wait(act, o_ln_done, m + 1)
                        wait(act, o_n_done, m)
                        act.activation(o_r[:, :], o_ln[:, :], ACT.Exp, scale=-0.5).then_inc(o_r_done, 1)
                    if e == 4 and nxt is not None:
                        wait(act, kg_exp_done, n + 1)
                        wait(act, log_g_done, n)
                        act.activation(kg_ln[:, :, :], kg_exp[:, :, :], ACT.Ln, bias=1.0).then_inc(kg_ln_done, 1)
                    if cur is not None and e == 7:
                        b = cur[0]
                        wait(act, gate_in_done, b + 1)
                        wait(act, gate_done, b)
                        act.activation(gate_t[:, :, :], gate_in[:, :, :], ACT.Tanh, scale=0.5).then_inc(gate_t_done, 1)
                    if prv is not None:
                        m, mh, mp = prv
                        if e == 1:
                            wait(act, o_done, 4 * m + 4)
                            wait(act, o_var_done, m)
                            act.activation(o_sq[:, :, :], o[:, :, :], ACT.Square).then_inc(o_sq_done, 1)
                        if e == 6:
                            wait(act, go_turned, m + 1)
                            wait(act, wo_done, m)
                            act.activation(go_t[:, :], turn_ps[:, :], ACT.Copy).then_inc(go_t_done, 1)
                        if e == 2:
                            wait(act, added, 8 * m + 8)
                            wait(act, fin2_done, m)
                            act.activation(sil_t[:, :], acc[mp][:, :, :].rearrange("p t d -> p (t d)"), ACT.Tanh,
                                           scale=0.5).then_inc(sil_done, 1)
                        if e == 7:
                            wait(act, wo_done, m + 1)
                            wait(act, fin1_done, m - 1)
                            act.activation(attn[mp][:, :], turn_ps[:, :], ACT.Copy).then_inc(attn_done, 1)

            phases(act, phase)

        @block.vector
        def _(dve):
            dve.wait_ge(w_small, 16 * 9)
            dve.tensor_reduce(vmean[:, :], wall[:, CV:CV + P].rearrange("p (h v) -> p h v", v=DV), AX_X,
                              ALU.add).then_inc(wprep, 1)
            dve.tensor_scalar(wall[:, CK:CK + KW], wall[:, CK:CK + KW], DK ** -0.5, None, ALU.mult).then_inc(wprep, 1)
            dve.wait_ge(wprep_pe, 1)
            dve.tensor_copy(wg1_t[:, :], turn_ps[0:16, 0:P]).then_inc(wprep, 1)
            dve.tensor_copy(wall[:, CR:CR + EXPERTS], turn_ps[:, P:P + EXPERTS]).then_inc(wprep, 1)
            dve.tensor_copy(bias[:, :], turn_ps[:, 2 * P:3 * P]).then_inc(wprep, 1)
            dve.wait_ge(wprep, 5)
            vv = wall[:, CV:CV + P].rearrange("p (h v) -> p h v", v=DV)
            dve.scalar_tensor_tensor(out=vv, in0=vmean[:, :].rearrange("p (h a) -> p h a", a=1).broadcast_to([P, HEADS, DV]),
                                     scalar=-1.0 / DV, in1=vv, op0=ALU.mult, op1=ALU.add).then_inc(wprep, 1)
            dve.wait_ge(wprep_pe, 2)
            dve.tensor_copy(wall[:, CG:CG + KW], proj_ps[:, 0:KW]).then_inc(wprep, 1)
            dve.wait_ge(consts, 16 + 5)
            dve.tensor_tensor(decay_sum[:, :], tri[:, :], first_half[:, :], ALU.subtract).then_inc(wprep, 1)
            dve.wait_ge(wprep, 8)
            dve.tensor_copy(wall_hi[:, :], wall[:, :]).then_inc(wprep, 1)
            dve.wait_ge(wprep, 9)
            dve.tensor_tensor(wall_lo[:, :], wall[:, :], wall_hi[:, :], ALU.subtract).then_inc(split_done, 1)
            def split_moe():
                dve.wait_ge(w_moe, 32)
                dve.tensor_copy(w1_hi[:, :, :], w1_raw[:, :, :]).then_inc(wprep, 1)
                dve.tensor_copy(w2_hi[:, :, :, :], w2_raw[:, :, :, :]).then_inc(wprep, 1)
                dve.wait_ge(wprep, 11)
                dve.tensor_tensor(w1_lo[:, :, :], w1_raw[:, :, :], w1_hi[:, :, :], ALU.subtract).then_inc(split_done, 1)
                dve.tensor_tensor(w2_lo[:, :, :, :], w2_raw[:, :, :, :], w2_hi[:, :, :, :],
                                  ALU.subtract).then_inc(split_done, 1)

            def layer_norm(n, half, par):
                wait(dve, x_loaded[par], 16 * (half + 1))
                wait(dve, ln_step, 3 * n - 1)
                wait(dve, xn_done, n)
                wait(dve, rstd_done, n)
                for j in range(TILES):
                    i = dve.bn_stats(stats[:, j, :], x_in[par][:, j, :])
                i.then_inc(ln_step, 1)
                wait(dve, ln_step, 3 * n + 1)
                dve.sem_inc(dve_past, 1)
                for j in range(TILES):
                    i = dve.bn_aggr(moments[:, j, :], stats[:, j, :])
                i.then_inc(ln_step, 1)
                wait(dve, ln_step, 3 * n + 2)
                dve.tensor_scalar(var_eps[:, :], moments[:, :, 1], EPS, None, ALU.add).then_inc(ln_step, 1)

            def normalise(n, half, par):
                wait(dve, rstd_done, n + 1)
                wait(dve, xt_turned, n)
                for j in range(TILES):
                    i = dve.tensor_scalar(xn[:, j, :], x_in[par][:, j, :], moments[:, j, 0:1], rstd[:, j:j + 1],
                                          ALU.subtract, ALU.mult)
                i.then_inc(xn_done, 1)

            def x_low(n, par):
                wait(dve, xt_hi_done, n + 1)
                dve.tensor_tensor(xt_lo[par][:, :], turn_ps[:, :], xt_hi[par][:, :], ALU.subtract).then_inc(xt_lo_done, 1)

            def router(n, par):
                wait(dve, proj_copied, 4 * n + 4)
                wait(dve, kg_exp_done, n)
                wait(dve, mix_done, n)
                wait(dve, gap_t_done, n)
                kg = proj[par][:, :, CG:CG + KW]
                dve.scalar_tensor_tensor(out=kg_neg[:, :, :], in0=kg, scalar=-1.0, in1=kg, op0=ALU.mult,
                                         op1=ALU.min).then_inc(kg_neg_done, 1)
                for j in range(TILES):
                    i = dve.max(top[:, j, :], proj[par][:, j, CR:CR + EXPERTS])
                i.then_inc(router_step, 1)
                wait(dve, router_step, 5 * n + 1)
                dve.tensor_tensor(gap[:, :], top[:, :, 1], top[:, :, 0], ALU.subtract).then_inc(gap_done, 1)
                for j in range(TILES):
                    i = dve.max_index(top_no[:, j, :], top[:, j, :], proj[par][:, j, CR:CR + EXPERTS])
                i.then_inc(router_step, 1)
                wait(dve, router_step, 5 * n + 2)
                dve.tensor_copy(top_nof[:, :, :], top_no[:, :, :]).then_inc(router_step, 1)
                wait(dve, router_step, 5 * n + 3)
                for k, pick in enumerate((pick1, pick2)):
                    i = dve.tensor_tensor(pick[:, :, :], expert_no[:, :, :],
                                          top_nof[:, :, k:k + 1].broadcast_to([P, TILES, EXPERTS]), ALU.is_equal)
                wait(dve, gap_t_done, n + 1)
                dve.tensor_scalar(p1[:, :], gap_t[:, :], -0.5, 0.5, ALU.mult, ALU.add)
                dve.tensor_scalar(p2[:, :], gap_t[:, :], 0.5, 0.5, ALU.mult, ALU.add).then_inc(router_step, 1)
                wait(dve, router_step, 5 * n + 4)
                for pick, pk in ((pick1, p1), (pick2, p2)):
                    i = dve.tensor_tensor(pick[:, :, :], pick[:, :, :],
                                          pk[:, :].rearrange("p (t a) -> p t a", a=1).broadcast_to([P, TILES, EXPERTS]), ALU.mult)
                i.then_inc(router_step, 1)
                wait(dve, router_step, 5 * n + 5)
                wait(dve, added, 8 * (n - 1))
                dve.tensor_tensor(mix[par][:, :, :], pick1[:, :, :], pick2[:, :, :], ALU.add).then_inc(mix_done, 1)

            def log_gate(n, par):
                wait(dve, kg_ln_done, n + 1)
                wait(dve, decay_done, n)
                dve.scalar_tensor_tensor(out=log_g[:, :, :], in0=proj[par][:, :, CG:CG + KW], scalar=0.0,
                                         in1=kg_ln[:, :, :], op0=ALU.min, op1=ALU.subtract).then_inc(log_g_done, 1)

            ORDER = (0, 2, 1, 3)

            def carry_on(b, bp, s):
                wait(dve, state_done, 4 * b + s + 1)
                wait(dve, state_done, 4 * (b - 1) + 4)
                dd = carry_dec[96:P, s, :].rearrange("p (h k a) -> p h k a", h=HEADS, a=1).broadcast_to([P - 96, HEADS, DK, DV])
                dve.tensor_tensor(carry[s][96:P, :].rearrange("p (h k v) -> p h k v", h=HEADS, k=DK),
                                  state_ps[s][96:P, :].rearrange("p (h k v) -> p h k v", h=HEADS, k=DK), dd,
                                  ALU.mult).then_inc(carry_done, 1)

            def read_state(b, bp, i):
                j = ORDER[i]
                wait(dve, o_done, 4 * b + i - 1)
                wait(dve, state_done, 4 * b + i + 1)
                wait(dve, q_done, b + 1)
                qq = q_dec[:, j, :].rearrange("p (h k a) -> p h k a", h=HEADS, a=1).broadcast_to([P, HEADS, DK, DV])
                dve.tensor_tensor(qs[i % 2][:, :].rearrange("p (h k v) -> p h k v", h=HEADS, k=DK),
                                  state_ps[j // 2][:, :].rearrange("p (h k v) -> p h k v", h=HEADS, k=DK), qq,
                                  ALU.mult).then_inc(qs_done, 1)

            def sum_keys(b, bp, i):
                j = ORDER[i]
                wait(dve, qs_done, 4 * b + i + 1)
                if i == 0:
                    wait(dve, o_n_done, b)
                dve.tensor_reduce(o[:, j, :].rearrange("p (h v) -> p h v", h=HEADS),
                                  qs[i % 2][:, :].rearrange("p (h k v) -> p h v k", h=HEADS, k=DK), AX_X,
                                  ALU.add).then_inc(o_done, 1)

            def head_var(b):
                wait(dve, o_sq_done, b + 1)
                wait(dve, o_ln_done, b)
                dve.tensor_reduce(o_var[:, :], o_sq[:, :, :].rearrange("p t (h v) -> p (t h) v", v=DV), AX_X,
                                  ALU.add).then_inc(o_var_done, 1)
                wait(dve, o_var_done, b + 1)
                dve.tensor_scalar(o_ve[:, :], o_var[:, :], 4.0 / DV, 4.0 * EPS, ALU.mult,
                                  ALU.add).then_inc(o_ve_done, 1)

            def gate_silu(b):
                wait(dve, gate_t_done, b + 1)
                wait(dve, go_done, b)
                dve.scalar_tensor_tensor(out=gate[:, :, :], in0=gate_t[:, :, :], scalar=1.0, in1=gate_in[:, :, :],
                                         op0=ALU.add, op1=ALU.mult).then_inc(gate_done, 1)

            def gated(b):
                wait(dve, o_r_done, b + 1)
                wait(dve, go_done, b)
                dve.tensor_tensor(o_n[:, :, :].rearrange("p t (h v) -> p (t h) v", v=DV),
                                  o[:, :, :].rearrange("p t (h v) -> p (t h) v", v=DV),
                                  o_r[:, :].rearrange("p (h a) -> p h a", a=1).broadcast_to([P, TILES * HEADS, DV]),
                                  ALU.mult).then_inc(o_n_done, 1)
                wait(dve, o_n_done, b + 1)
                wait(dve, gate_done, b + 1)
                wait(dve, go_turned, b)
                dve.tensor_tensor(go[:, :, :], o_n[:, :, :], gate[:, :, :], ALU.mult).then_inc(go_done, 1)

            def low(b, e):
                for f in range(FH):
                    h = 2 * e + f
                    wait(dve, gelu_done, 16 * b + h + 1)
                    wait(dve, down_done, 8 * b + e - 1)
                    dve.tensor_tensor(h_lo[h % 4][:, :], h_act[f][:, :], h_hi[h % 4][:, :],
                                      ALU.subtract).then_inc(lo_done, 1)

            def add_expert(b, bp, e):
                wait(dve, down_done, 8 * b + e + 1)
                if e == 0:
                    wait(dve, mix_done, b + 1)
                    wait(dve, fin1_done, b - 1)
                else:
                    wait(dve, added, 8 * b + e)
                for j in range(TILES):
                    y, w = y_ps[e % 2][:, j * P:(j + 1) * P], mix[bp][:, j, e:e + 1]
                    if e == 0:
                        i = dve.tensor_scalar(acc[bp][:, j, :], y, w, None, ALU.mult)
                    else:
                        i = dve.scalar_tensor_tensor(out=acc[bp][:, j, :], in0=y, scalar=w, in1=acc[bp][:, j, :],
                                                     op0=ALU.mult, op1=ALU.add)
                i.then_inc(added, 1)

            def finish(b, bh, bp):
                wait(dve, attn_done, b + 1)
                wait(dve, out_done, b)
                wait(dve, added, 8 * b + 8)
                dve.tensor_tensor(fin1[:, :], acc[bp][:, :, :].rearrange("p t d -> p (t d)"), attn[bp][:, :],
                                  ALU.mult).then_inc(fin1_done, 1)
                wait(dve, fin1_done, b + 1)
                wait(dve, sil_done, b + 1)
                dve.scalar_tensor_tensor(out=fin2[:, :], in0=sil_t[:, :], scalar=1.0, in1=fin1[:, :], op0=ALU.add,
                                         op1=ALU.mult).then_inc(fin2_done, 1)
                wait(dve, fin2_done, b + 1)
                wait(dve, res_loaded[bp], 16 * (bh + 1))
                wait(dve, stored[bp], 16 * bh)
                dve.scalar_tensor_tensor(out=y_out[bp][:, :, :].rearrange("p t d -> p (t d)"), in0=fin2[:, :],
                                         scalar=0.5, in1=x_res[bp][:, :, :].rearrange("p t d -> p (t d)"),
                                         op0=ALU.mult, op1=ALU.add).then_inc(out_done, 1)

            def phase(prv, cur, nxt):
                for e in range(EXPERTS):
                    if nxt is not None and e == 0:
                        layer_norm(*nxt)
                    if prv is not None and e == 0:
                        m, mh, mp = prv
                        if not (isinstance(m, int) and m == 0):
                            finish(m - 1, mh - 1 + mp, 1 - mp)
                    if cur is not None:
                        b, bh, bp = cur
                        low(b, e)
                        if e:
                            add_expert(b, bp, e - 1)
                    if prv is not None and e == 0:
                        add_expert(m, mp, EXPERTS - 1)
                    if nxt is not None:
                        n, half, par = nxt
                        if e == 0:
                            normalise(n, half, par)
                        if e == 1:
                            x_low(n, par)
                        if e == 4:
                            router(n, par)
                        if e == 5:
                            log_gate(n, par)
                    if prv is not None:
                        if e == 0:
                            sum_keys(m, mp, 2)
                            sum_keys(m, mp, 3)
                        if e == 1:
                            gate_silu(m)
                        if e == 2:
                            head_var(m)
                        if e == 5:
                            gated(m)
                    if cur is not None:
                        if e == 6:
                            carry_on(b, bp, 0)
                            carry_on(b, bp, 1)
                            read_state(b, bp, 0)
                            read_state(b, bp, 1)
                        if e == 7:
                            sum_keys(b, bp, 0)
                            sum_keys(b, bp, 1)
                            read_state(b, bp, 2)
                            read_state(b, bp, 3)
                    elif e == 4 and nxt is not None:
                        split_moe()

            phases(dve, phase)
            finish(blocks - 1, blocks // 2 - 1, 1)

        @block.tensor
        def _(pe):
            pe.wait_ge(consts, 16 + 5)
            pe.wait_ge(ones_made, 1)
            pe.wait_ge(w_small, 16 * 9)
            pe.transpose(turn_ps[0:16, 0:P], wg1_in[:, :], ident[:, :])
            pe.transpose(turn_ps[:, P:P + EXPERTS], router_in[:, :], ident[0:EXPERTS, 0:EXPERTS])
            pe.matmul(turn_ps[:, 2 * P:3 * P], ones_row[:, :], bg_row[:, :], start=True, stop=True).then_inc(wprep_pe, 1)
            pe.wait_ge(wprep, 5)
            pe.matmul(proj_ps[:, 0:KW], wg1_t[:, :], wg2_in[:, :], start=True, stop=True).then_inc(wprep_pe, 1)
            pe.wait_ge(split_done, 1)

            def three(dst, a_hi, a_lo, b_hi, b_lo, start=True, stop=True):
                pe.matmul(dst, a_hi, b_hi, start=start, stop=False)
                pe.matmul(dst, a_hi, b_lo, start=False, stop=False)
                return pe.matmul(dst, a_lo, b_hi, start=False, stop=stop)

            def up(b, bp, e):
                if e == 0:
                    wait(pe, xt_lo_done, b + 1)
                    if isinstance(b, int) and b == 0:
                        pe.wait_ge(split_done, 3)
                for f in range(FH):
                    h = 2 * e + f
                    wait(pe, gelu_done, 16 * b + h - 1)
                    c = slice(f * P, (f + 1) * P)
                    three(h_ps[f][:, :], w1_hi[:, e, c], w1_lo[:, e, c], xt_hi[bp][:, :],
                          xt_lo[bp][:, :]).then_inc(up_done, 1)

            def down(b, e):
                wait(pe, lo_done, 16 * b + 2 * e + 2)
                wait(pe, added, 8 * b + e - 1)
                for j in range(TILES):
                    c = slice(j * P, (j + 1) * P)
                    for f in range(FH):
                        h = (2 * e + f) % 4
                        i = three(y_ps[e % 2][:, c], h_hi[h][:, c], h_lo[h][:, c], w2_hi[:, e, f, :],
                                  w2_lo[:, e, f, :], start=(f == 0), stop=(f == FH - 1))
                i.then_inc(down_done, 1)

            def project(n, par, j):
                if j == 0:
                    wait(pe, xt_lo_done, n + 1)
                    wait(pe, e_done, 3 * (n - 1))
                else:
                    wait(pe, proj_copied, 4 * n + j)
                c = slice(j * P, (j + 1) * P)
                three(proj_ps[:, 0:CW], xt_hi[par][:, c], xt_lo[par][:, c], wall_hi[:, :],
                      wall_lo[:, :]).then_inc(proj_done, 1)

            def states(b, i, j):
                wait(pe, kv_done, 4 * b + i + 1)
                s = j // 2
                if i < 2:
                    wait(pe, qs_done, 4 * (b - 1) + i + 3)
                    pe.matmul(state_ps[s][:, :], tri[:, :], kv[j][:, :], start=True, stop=True).then_inc(state_done, 1)
                else:
                    wait(pe, qs_done, 4 * b + i - 1)
                    wait(pe, carry_done, 2 * b + s + 1)
                    pe.matmul(state_ps[s][:, :], tri[:, :], kv[j][:, :], start=True, stop=False)
                    pe.matmul(state_ps[s][:, :], last_row[:, :], carry[s][:, :], start=False,
                              stop=True).then_inc(state_done, 1)

            def phase(prv, cur, nxt):
                for e in range(EXPERTS):
                    if cur is not None:
                        up(cur[0], cur[2], e)
                    if nxt is not None and e == 1:
                        n, half, par = nxt
                        wait(pe, xn_done, n + 1)
                        wait(pe, attn_done, n - 2)
                        for j in range(TILES):
                            i = pe.transpose(turn_ps[:, j * P:(j + 1) * P], xn[:, j, :], ident[:, :])
                        i.then_inc(xt_turned, 1)
                    if nxt is not None and e in (2, 3):
                        project(n, par, 2 * e - 4)
                        project(n, par, 2 * e - 3)
                    if cur is not None:
                        b = cur[0]
                        if e == 4:
                            wait(pe, log_g_done, b + 1)
                            wait(pe, proj_copied, 4 * b + (8 if nxt is not None else 4))
                            pe.matmul(proj_ps[:, 0:TILES * KW], decay_sum[:, :],
                                      log_g[:, :, :].rearrange("p t k -> p (t k)"), start=True, stop=True)
                            dst = proj_ps[:, TILES * KW:(TILES + 2) * KW].rearrange("p (s k) -> p s k", s=2)
                            pe.matmul(dst, second_half[:, :], log_g[:, 0:TILES:2, :], start=True, stop=False)
                            pe.matmul(dst, first_half[:, :], log_g[:, 1:TILES:2, :], start=False,
                                      stop=True).then_inc(decay_done, 1)
                        if e:
                            down(b, e - 1)
                        if e == 6:
                            states(b, 0, 0)
                            states(b, 1, 2)
                        if e == 7:
                            states(b, 2, 1)
                            states(b, 3, 3)
                    if prv is not None:
                        m = prv[0]
                        if e == 0:
                            down(m, EXPERTS - 1)
                        if e == 6:
                            wait(pe, go_done, m + 1)
                            wait(pe, xt_lo_done, m + (3 if nxt is not None else 2 if cur is not None else 1))
                            for j in range(TILES):
                                i = pe.transpose(turn_ps[:, j * P:(j + 1) * P], go[:, j, :], ident[:, :])
                            i.then_inc(go_turned, 1)
                        if e == 7:
                            wait(pe, go_t_done, m + 1)
                            for j in range(TILES):
                                c = slice(j * P, (j + 1) * P)
                                i = pe.matmul(turn_ps[:, c], go_t[:, c], wo[:, :], start=True, stop=True)
                            i.then_inc(wo_done, 1)

            phases(pe, phase)


_INS = ['L0_attn_inputs', 'L0_attn_Wq', 'L0_attn_Wk', 'L0_attn_Wg1', 'L0_attn_Wg2', 'L0_attn_Wv', 'L0_attn_Wg',
        'L0_attn_bg', 'L0_attn_Wo', 'L0_ffn_router_w', 'L0_ffn_w1', 'L0_ffn_w2']
_OUTS = [((32, 256, 128), 'float32')]


def kernel(**inputs):
    import numpy as _np
    import concourse.bacc as _bacc
    from concourse import mybir as _mybir
    from concourse.bass_utils import run_bass_kernel_spmd as _run

    nc = _bacc.Bacc("TRN2", target_bir_lowering=False, num_devices=1)
    arrays, args = {}, []
    for name in _INS:
        a = _np.ascontiguousarray(inputs[name])
        arrays[f"in_{name}_dram"] = a
        args.append(nc.dram_tensor(f"in_{name}_dram", a.shape, _mybir.dt.from_np(a.dtype), kind="ExternalInput").ap())
    for i, (shape, dtype) in enumerate(_OUTS):
        dt = _mybir.dt.from_np(_np.dtype(dtype))
        args.append(nc.dram_tensor(f"out_{i}_dram", shape, dt, kind="ExternalOutput").ap())
    gla_moe_kernel(nc, *args)
    r = _run(nc, [arrays], core_ids=[0])
    got = tuple(r.results[0][f"out_{i}_dram"] for i in range(len(_OUTS)))
    return got[0]
```

```python
from contextlib import ExitStack

import concourse.bass as bass
from concourse import mybir

ALU = mybir.AluOpType
ACT = mybir.ActivationFunctionType
AX_X = mybir.AxisListType.X
F32 = mybir.dt.float32
F16 = mybir.dt.float16
U32 = mybir.dt.uint32

P = 128
TILES = 4
TOK = TILES * P
HEADS, DK, DV = 16, 4, 8
KW = HEADS * DK
SW = HEADS * DK * DV
EXPERTS = 8
FH = 2
GATE_NORM = 16.0
EPS = 1e-5
CQ, CK, CG, CR, CV, CO, CW = 0, 64, 128, 192, 200, 328, 456


def gla_moe_kernel(nc, x, Wq, Wk, Wg1, Wg2, Wv, Wg, bg, Wo, router_w, w1, w2, out):
    blocks = x.shape[0] * x.shape[1] // TOK
    assert blocks % 2 == 0 and blocks >= 8
    xb = x.rearrange("(n s) (c p) d -> n c p s d", s=2, p=P)
    ob = out.rearrange("(n s) (c p) d -> n c p s d", s=2, p=P)

    def pieces(dram, n, tiles):
        return ((dram[n, 0, 0:P - 1], tiles[1:P, 0:TILES:2, :]), (dram[n, 0, P - 1:P], tiles[0:1, 0:TILES:2, :]),
                (dram[n, 1], tiles[:, 1:TILES:2, :]))
    PIECES = 3

    with ExitStack() as ctx:
        def sb(name, shape, dt=F32):
            return ctx.enter_context(nc.sbuf_tensor(name, shape, dt))

        def sem(name):
            return ctx.enter_context(nc.semaphore(name))

        def ps(name):
            return ctx.enter_context(nc.psum_tensor(name, [P, 512], F32))

        h_ps = [ps(f"h_ps{i}") for i in range(4)]
        y_ps = [ps(f"y_ps{i}") for i in range(2)]
        state_ps = ps("state_ps")
        misc_ps = ps("misc_ps")

        wall = sb("wall", [P, CW])
        wall_hi, wall_lo = sb("wall_hi", [P, CW], F16), sb("wall_lo", [P, CW], F16)
        w1_raw, w2_raw = sb("w1_raw", [P, EXPERTS, 256]), sb("w2_raw", [P, EXPERTS, FH, P])
        w1_hi, w1_lo = sb("w1_hi", [P, EXPERTS, 256], F16), sb("w1_lo", [P, EXPERTS, 256], F16)
        w2_hi, w2_lo = sb("w2_hi", [P, EXPERTS, FH, P], F16), sb("w2_lo", [P, EXPERTS, FH, P], F16)
        wo = sb("wo", [P, P])
        wg1_in, wg2_in, router_in = sb("wg1_in", [P, 16]), sb("wg2_in", [16, KW]), sb("router_in", [EXPERTS, P])
        wg1_t = sb("wg1_t", [16, P])
        vmean = sb("vmean", [P, HEADS])
        bg_row, ones_row, bias = sb("bg_row", [1, P]), sb("ones_row", [1, P]), sb("bias", [P, P])
        ident = sb("ident", [P, P])
        tri, first_half, decay_sum = ([sb(f"{n}{i}", [P, P]) for i in range(2)] for n in ("tri", "first_half", "decay_sum"))
        expert_no = sb("expert_no", [P, TILES, EXPERTS])
        minus_half = sb("minus_half", [P, TILES * HEADS])

        x_in = [sb(f"x_in{i}", [P, TILES, P]) for i in range(2)]
        x_res = [sb(f"x_res{i}", [P, TILES, P]) for i in range(2)]
        y_out = [sb(f"y_out{i}", [P, TILES, P]) for i in range(2)]
        acc = [sb(f"acc{i}", [P, TILES, P]) for i in range(2)]
        attn = [sb(f"attn{i}", [P, TOK]) for i in range(2)]
        xt_hi = [sb(f"xt_hi{i}", [P, TOK], F16) for i in range(2)]
        xt_lo = [sb(f"xt_lo{i}", [P, TOK], F16) for i in range(2)]
        proj = [sb(f"proj{i}", [P, TILES, CW]) for i in range(2)]
        q_dec, k_dec, carry_dec = sb("q_dec", [P, TILES, KW]), sb("k_dec", [P, TILES, KW]), sb("carry_dec", [1, 2, KW])
        g_first, carry_half = sb("g_first", [1, 2, KW]), sb("carry_half", [1, 2, KW])
        mix = [sb(f"mix{i}", [P, TILES, EXPERTS]) for i in range(2)]
        stats, moments = sb("stats", [P, TILES, 6]), sb("moments", [P, TILES, 2])
        var_eps, rstd, shift = (sb(n, [P, TILES]) for n in ("var_eps", "rstd", "shift"))
        xn = sb("xn", [P, TILES, P])
        kg_neg, kg_exp, kg_ln, log_g = (sb(n, [P, TILES, KW]) for n in ("kg_neg", "kg_exp", "kg_ln", "log_g"))
        e_pos, e_neg = sb("e_pos", [P, TILES, KW]), sb("e_neg", [P, TILES, KW])
        top, top_no = sb("top", [P, TILES, 8]), sb("top_no", [P, TILES, 8], U32)
        top_nof, gap, gap_t = sb("top_nof", [P, TILES, 8]), sb("gap", [P, TILES]), sb("gap_t", [P, TILES])
        p1, p2 = sb("p1", [P, TILES]), sb("p2", [P, TILES])
        pick1, pick2 = sb("pick1", [P, TILES, EXPERTS]), sb("pick2", [P, TILES, EXPERTS])
        kv = [sb(f"kv{i}", [P, SW]) for i in range(4)]
        carry = [sb(f"carry{i}", [1, SW]) for i in range(2)]
        qs = [sb(f"qs{i}", [P, SW]) for i in range(2)]
        o, o_sq = sb("o", [P, TILES, P]), sb("o_sq", [P, TILES, P])
        o_var, o_r = sb("o_var", [P, TILES * HEADS]), sb("o_r", [P, TILES * HEADS])
        o_ve, o_ln = sb("o_ve", [P, TILES * HEADS]), sb("o_ln", [P, TILES * HEADS])
        gate_in, gate_t, gate = (sb(n, [P, TILES, P]) for n in ("gate_in", "gate_t", "gate"))
        o_n, go = sb("o_n", [P, TILES, P]), sb("go", [P, TILES, P])
        go_t = sb("go_t", [P, TOK])
        sil_t, fin1, fin2 = (sb(n, [P, TOK]) for n in ("sil_t", "fin1", "fin2"))
        h_act = [[sb(f"h_act{i}{f}", [P, TOK]) for f in range(FH)] for i in range(2)]
        h_hi = [[sb(f"h_hi{i}{f}", [P, TOK], F16) for f in range(FH)] for i in range(4)]
        h_lo = [[sb(f"h_lo{i}{f}", [P, TOK], F16) for f in range(FH)] for i in range(4)]

        w_small, w1_loaded, w2_loaded, consts, ones_made = (
            sem("w_small"), sem("w1_loaded"), sem("w2_loaded"), sem("consts"), sem("ones_made"))
        w1_high, w2_high, w1_split, w2_split = sem("w1_high"), sem("w2_high"), sem("w1_split"), sem("w2_split")
        wprep, wprep_pe, split_done = sem("wprep"), sem("wprep_pe"), sem("split_done")
        dve_past = sem("dve_past")
        x_loaded = [sem(f"x_loaded{i}") for i in range(2)]
        res_loaded = [sem(f"res_loaded{i}") for i in range(2)]
        stored = [sem(f"stored{i}") for i in range(2)]
        ln_step, rstd_done, shift_done, xn_done = sem("ln_step"), sem("rstd_done"), sem("shift_done"), sem("xn_done")
        xt_turned, xt_hi_done, xt_lo_done = sem("xt_turned"), sem("xt_hi_done"), sem("xt_lo_done")
        proj_done, proj_copied = sem("proj_done"), sem("proj_copied")
        router_step, gap_done, gap_t_done, mix_done = sem("router_step"), sem("gap_done"), sem("gap_t_done"), sem("mix_done")
        kg_neg_done, kg_exp_done, kg_ln_done, log_g_done = (
            sem("kg_neg_done"), sem("kg_exp_done"), sem("kg_ln_done"), sem("log_g_done"))
        decay_done, e_done, q_done, k_done = sem("decay_done"), sem("e_done"), sem("q_done"), sem("k_done")
        kv_done, state_done, carry_done = sem("kv_done"), sem("state_done"), sem("carry_done")
        kv_joined, decayed = sem("kv_joined"), sem("decayed")
        qs_done, o_done, o_sq_done, o_var_done, o_ve_done, o_ln_done, o_r_done = (
            sem("qs_done"), sem("o_done"), sem("o_sq_done"), sem("o_var_done"), sem("o_ve_done"), sem("o_ln_done"),
            sem("o_r_done"))
        gate_in_done, gate_t_done, gate_done, o_n_done, go_done = (
            sem("gate_in_done"), sem("gate_t_done"), sem("gate_done"), sem("o_n_done"), sem("go_done"))
        go_turned, go_t_done, wo_done, attn_done = sem("go_turned"), sem("go_t_done"), sem("wo_done"), sem("attn_done")
        up_done, gelu_done = sem("up_done"), sem("gelu_done")
        lo_done = [sem(f"lo_done{f}") for f in range(FH)]
        down_done, added = sem("down_done"), sem("added")
        sil_done, fin1_done, fin2_done, out_done = sem("sil_done"), sem("fin1_done"), sem("fin2_done"), sem("out_done")

        PROJ_SLOTS = (0, 1, 4, 5)
        STATE_SLOTS = (0, 2, 3, 4)
        ORDER = (0, 2, 1, 3)
        CONSTS = 6 + EXPERTS + 5 + 3

        def wait(eng, s, value):
            if not isinstance(value, int) or value > 0:
                eng.wait_ge(s, value)

        def proj_bank(n, i):
            return h_ps[i] if isinstance(n, int) and n == 0 else misc_ps

        def phases(eng, phase):
            def run(pair, k, least, most):
                def at(d):
                    i = k + d
                    return (2 * pair + i, pair + i // 2, i % 2) if least <= d <= most else None
                phase(at)
            run(0, -2, 2, 2)
            run(0, -1, 1, 2)
            run(0, 0, 0, 2)
            run(0, 1, -1, 2)
            run(0, 2, -2, 2)
            with eng.Fori(1, blocks // 2 - 2) as pair:
                run(pair, 1, -2, 2)
                run(pair, 2, -2, 2)
            run(0, blocks - 3, -2, 2)
            run(0, blocks - 2, -2, 1)
            run(0, blocks - 1, -2, 0)
            run(0, blocks, -2, -1)
            run(0, blocks + 1, -2, -2)

        block = ctx.enter_context(nc.Block())

        @block.sync
        def _(sp):
            for src, dst in pieces(xb, 0, x_in[0]):
                sp.dma_start(dst, src).then_inc(x_loaded[0], 16)
            for dst, src in ((wall[:, CQ:CQ + KW], Wq), (wall[:, CK:CK + KW], Wk), (wall[:, CV:CV + P], Wv),
                             (wall[:, CO:CO + P], Wg), (wg1_in[:, :], Wg1), (wg2_in[:, :], Wg2),
                             (router_in[:, :], router_w), (wo[:, :], Wo),
                             (bg_row[:, :], bg.rearrange("(a n) -> a n", a=1))):
                sp.dma_start(dst, src).then_inc(w_small, 16)
            sp.dma_start(w1_raw[:, :, :], w1.rearrange("e d f -> d e f")).then_inc(w1_loaded, 16)
            sp.dma_start(w2_raw[:, :, :, :], w2.rearrange("e (h p) d -> p e h d", p=P)).then_inc(w2_loaded, 16)

            def phase(at):
                if at(2) and not (isinstance(at(2)[0], int) and at(2)[0] == 0):
                    n, half, par = at(2)
                    wait(sp, xn_done, n - 1)
                    for src, dst in pieces(xb, n, x_in[par]):
                        sp.dma_start(dst, src).then_inc(x_loaded[par], 16)
                if at(-1):
                    m, mh, mp = at(-1)
                    wait(sp, out_done, m - 1)
                    for src, dst in pieces(xb, m, x_res[mp]):
                        sp.dma_start(dst, src).then_inc(res_loaded[mp], 16)
                if at(-2):
                    b, bh, bp = at(-2)
                    wait(sp, out_done, b + 1)
                    for dst, src in pieces(ob, b, y_out[bp]):
                        sp.dma_start(dst, src).then_inc(stored[bp], 16)

            phases(sp, phase)
            sp.wait_ge(stored[0], 16 * PIECES * (blocks // 2))
            sp.wait_ge(stored[1], 16 * PIECES * (blocks // 2))

        @block.gpsimd
        def _(pool):
            pool.memset(ones_row[:, :], 1.0).then_inc(ones_made, 1)
            made = 0
            for m, v in ((ident, 0.0), (tri[0], 1.0), (tri[1], 1.0), (first_half[0], 1.0), (first_half[1], 1.0),
                         (minus_half, -0.5)):
                pool.memset(m[:, :], v).then_inc(consts, 1)
                made += 1
            for e in range(EXPERTS):
                pool.memset(expert_no[:, :, e:e + 1], float(e)).then_inc(consts, 1)
                made += 1
            pool.wait_ge(consts, made)
            for m, op, base, rows, cols, fill in (
                    (ident, ALU.not_equal, 0, 1, -1, 1.0),
                    (tri[0], ALU.is_ge, 0, -1, 1, 0.0),
                    (tri[1], ALU.is_ge, 0, -1, 1, 0.0),
                    (first_half[0], ALU.is_ge, P // 2, -1, 0, 0.0),
                    (first_half[1], ALU.is_ge, P // 2 - 1, -1, 0, 0.0)):
                pool.affine_select(out=m[:, :], in_=m[:, :], compare_op=op, fill=fill, base=base,
                                   pattern=[[cols, P]], channel_multiplier=rows).then_inc(consts, 1)
                made += 1
            pool.wait_ge(consts, made)
            for rows, v in ((tri[0][0:1, 1:P], 0.0), (tri[0][:, 0:1], 1.0), (first_half[0][0:1, :], 0.0)):
                pool.memset(rows, v).then_inc(consts, 1)
                made += 1
            assert made == CONSTS

            def outer(b, bp, i):
                j = ORDER[i]
                if i == 0:
                    wait(pool, k_done, b + 1)
                    wait(pool, state_done, 4 * b)
                kk = k_dec[:, j, :].rearrange("p (h k a) -> p h k a", h=HEADS, a=1).broadcast_to([P, HEADS, DK, DV])
                vv = proj[bp][:, j, CV:CV + P].rearrange("p (h a v) -> p h a v", h=HEADS, a=1).broadcast_to([P, HEADS, DK, DV])
                pool.tensor_tensor(kv[j][:, :].rearrange("p (h k v) -> p h k v", h=HEADS, k=DK), kk, vv,
                                   ALU.mult).then_inc(kv_done, 1)

            def join(b, s):
                wait(pool, carry_done, 2 * b + s + 1)
                wait(pool, kv_done, 4 * b + 3 + s)
                pool.tensor_tensor(kv[2 * s + 1][0:1, :], kv[2 * s + 1][0:1, :], carry[s][:, :],
                                   ALU.add).then_inc(kv_joined, 1)

            def low(b, e):
                h = h_act[e % 2][1]
                wait(pool, down_done, 8 * b + e - 3)
                wait(pool, gelu_done, 16 * b + 2 * e + 2)
                pool.tensor_tensor(h_lo[e % 4][1][:, :], h[:, :], h_hi[e % 4][1][:, :],
                                   ALU.subtract).then_inc(lo_done[1], 1)

            def phase(at):
                for e in range(EXPERTS):
                    if at(1) and not at(0) and e == 5:
                        pool.wait_ge(w2_high, 1)
                        pool.tensor_tensor(w2_lo[:, :, :, :], w2_raw[:, :, :, :], w2_hi[:, :, :, :],
                                           ALU.subtract).then_inc(w2_split, 1)
                    if at(2) and e == 2:
                        n, half, par = at(2)
                        wait(pool, ln_step, 3 * n + 3)
                        wait(pool, xn_done, n)
                        pool.tensor_tensor(rstd[:, :], var_eps[:, :], minus_half[:, 0:TILES],
                                           ALU.pow).then_inc(rstd_done, 1)
                    if at(0):
                        low(at(0)[0], e)
                    if at(-1) and e < 2:
                        m, mh, mp = at(-1)
                        outer(m, mp, 2 + e)
                    if at(-1) and e in (1, 2):
                        join(m, e - 1)
                    if at(-1) and e == 7:
                        m = at(-1)[0]
                        wait(pool, o_n_done, m + 1)
                        wait(pool, gate_done, m + 1)
                        wait(pool, go_turned, m)
                        pool.tensor_tensor(go[:, :, :], o_n[:, :, :], gate[:, :, :], ALU.mult).then_inc(go_done, 1)
                    if at(-2) and e == 3:
                        m2, _, bp = at(-2)
                        wait(pool, attn_done, m2 + 1)
                        wait(pool, added, 8 * m2 + 8)
                        wait(pool, fin2_done, m2)
                        pool.tensor_tensor(fin1[:, :], acc[bp][:, :, :].rearrange("p t d -> p (t d)"), attn[bp][:, :],
                                           ALU.mult).then_inc(fin1_done, 1)
                    if at(0) and e == 5:
                        b, bh, bp = at(0)
                        wait(pool, gate_done, b)
                        pool.tensor_tensor(gate_in[:, :, :], proj[bp][:, :, CO:CO + P],
                                           bias[:, :].rearrange("p (a n) -> p a n", a=1).broadcast_to([P, TILES, P]),
                                           ALU.add).then_inc(gate_in_done, 1)
                    if at(0) and e == 6:
                        b, bh, bp = at(0)
                        wait(pool, e_done, 3 * b + 3)
                        wait(pool, qs_done, 4 * b)
                        pool.tensor_tensor(k_dec[:, :, :], proj[bp][:, :, CK:CK + KW], e_neg[:, :, :],
                                           ALU.mult).then_inc(k_done, 1)
                        outer(b, bp, 0)
                        pool.tensor_tensor(q_dec[:, :, :], proj[bp][:, :, CQ:CQ + KW], e_pos[:, :, :],
                                           ALU.mult).then_inc(q_done, 1)
                    if at(0) and e == 7:
                        outer(b, bp, 1)

            phases(pool, phase)

        @block.scalar
        def _(act):
            def gelu(b, e):
                for f in range(FH):
                    wait(act, up_done, 16 * b + 2 * e + f + 1)
                    wait(act, down_done, 8 * b + e - 3)
                    wait(act, lo_done[f], 8 * b + e - 1)
                    act.activation(h_hi[e % 4][f][:, :], h_ps[e % 2 * 2 + f][:, :], ACT.Gelu)
                    act.activation(h_act[e % 2][f][:, :], h_ps[e % 2 * 2 + f][:, :], ACT.Gelu).then_inc(gelu_done, 1)

            def exponentials(m, b, n):
                act.preload_act_table_set("natural_log_exp_and_others")
                if m is not None:
                    wait(act, o_ve_done, m + 1)
                    wait(act, o_r_done, m)
                    act.activation(o_ln[:, :], o_ve[:, :], ACT.Ln).then_inc(o_ln_done, 1)
                if n is not None:
                    wait(act, kg_neg_done, n + 1)
                    wait(act, kg_ln_done, n)
                    act.activation(kg_exp[:, :, :], kg_neg[:, :, :], ACT.Exp).then_inc(kg_exp_done, 1)
                if b is not None:
                    wait(act, decay_done, b + 1)
                    wait(act, q_done, b)
                    wait(act, decayed, 2 * b)
                    dec = misc_ps[:, 0:TILES * KW].rearrange("p (t k) -> p t k", t=TILES)
                    act.activation(e_neg[:, :, :], dec, ACT.Exp, scale=-1.0 / GATE_NORM).then_inc(e_done, 1)
                    act.activation(e_pos[:, :, :], dec, ACT.Exp, scale=1.0 / GATE_NORM).then_inc(e_done, 1)
                    act.activation(g_first[:, :, :], log_g[0:1, 1:TILES:2, :], ACT.Exp,
                                   scale=1.0 / GATE_NORM).then_inc(e_done, 1)
                if m is not None:
                    wait(act, o_ln_done, m + 1)
                    wait(act, o_n_done, m)
                    act.activation(o_r[:, :], o_ln[:, :], ACT.Exp, scale=-0.5).then_inc(o_r_done, 1)
                if n is not None:
                    wait(act, kg_exp_done, n + 1)
                    wait(act, log_g_done, n)
                    act.activation(kg_ln[:, :, :], kg_exp[:, :, :], ACT.Ln, bias=1.0).then_inc(kg_ln_done, 1)

            def phase(at):
                for e in range(EXPERTS):
                    if at(1) and not at(0) and e == 0:
                        act.wait_ge(w1_loaded, 16)
                        act.activation(w1_hi[:, :, :], w1_raw[:, :, :], ACT.Copy).then_inc(w1_high, 1)
                    if at(1) and not at(0) and e == 5:
                        act.wait_ge(w2_loaded, 16)
                        act.activation(w2_hi[:, :, :, :], w2_raw[:, :, :, :], ACT.Copy).then_inc(w2_high, 1)
                    if at(2) and e == 4:
                        n, half, par = at(2)
                        wait(act, shift_done, n + 1)
                        wait(act, xt_turned, n)
                        for j in range(TILES):
                            i = act.activation(xn[:, j, :], x_in[par][:, j, :], ACT.Identity, bias=shift[:, j:j + 1],
                                               scale=rstd[:, j:j + 1])
                        i.then_inc(xn_done, 1)
                    if at(-1) and e == 6:
                        m = at(-1)[0]
                        wait(act, o_done, 4 * m + 4)
                        wait(act, o_var_done, m)
                        act.activation(o_sq[:, :, :], o[:, :, :], ACT.Square).then_inc(o_sq_done, 1)
                    if at(2):
                        n, half, par = at(2)
                        if e == 7:
                            wait(act, xt_turned, n + 1)
                            wait(act, up_done, 16 * (n - 1))
                            wait(act, proj_done, 4 * (n - 1))
                            act.activation(xt_hi[par][:, :], misc_ps[:, :], ACT.Copy).then_inc(xt_hi_done, 1)
                    if at(0):
                        b = at(0)[0]
                        gelu(b, e)
                    if at(-2):
                        m2, _, bp = at(-2)
                        if e == 1:
                            wait(act, added, 8 * m2 + 8)
                            wait(act, fin2_done, m2)
                            act.activation(sil_t[:, :], acc[bp][:, :, :].rearrange("p t d -> p (t d)"), ACT.Tanh,
                                           scale=0.5).then_inc(sil_done, 1)
                        if e == 2:
                            wait(act, go_turned, m2 + 1)
                            wait(act, wo_done, m2)
                            act.activation(go_t[:, :], misc_ps[:, :], ACT.Copy).then_inc(go_t_done, 1)
                        if e == 3:
                            wait(act, wo_done, m2 + 1)
                            wait(act, fin1_done, m2 - 1)
                            act.activation(attn[bp][:, :], misc_ps[:, :], ACT.Copy).then_inc(attn_done, 1)
                    if at(-1):
                        m, _, mp = at(-1)
                        if e == 0:
                            wait(act, gate_in_done, m + 1)
                            wait(act, gate_done, m)
                            act.activation(gate_t[:, :, :], gate_in[:, :, :], ACT.Tanh, scale=0.5).then_inc(gate_t_done, 1)
                    if at(1):
                        n, half, par = at(1)
                        if e in PROJ_SLOTS:
                            i = PROJ_SLOTS.index(e)
                            wait(act, proj_done, 4 * n + i + 1)
                            wait(act, kv_done, 4 * (n - 2) + i + 1)
                            if i == 0:
                                wait(act, gate_in_done, n - 1)
                                wait(act, mix_done, n - 1)
                                wait(act, q_done, n - 1)
                                wait(act, log_g_done, n - 1)
                            act.activation(proj[par][:, ORDER[i], :], proj_bank(n, i)[:, 0:CW], ACT.Copy).then_inc(proj_copied, 1)
                        if e == 7:
                            wait(act, gap_done, n + 1)
                            wait(act, router_step, 5 * n - 1)
                            act.activation(gap_t[:, :], gap[:, :], ACT.Tanh, scale=0.5).then_inc(gap_t_done, 1)
                    if e == 6 and (at(-1) or at(1)):
                        exponentials(*(at(d)[0] if at(d) else None for d in (-1, 0, 1)))

            phases(act, phase)

        @block.vector
        def _(dve):
            def split_small():
                dve.wait_ge(w_small, 16 * 9)
                dve.tensor_reduce(vmean[:, :], wall[:, CV:CV + P].rearrange("p (h v) -> p h v", v=DV), AX_X,
                                  ALU.add).then_inc(wprep, 1)
                dve.tensor_scalar(wall[:, CK:CK + KW], wall[:, CK:CK + KW], DK ** -0.5, None, ALU.mult).then_inc(wprep, 1)
                dve.wait_ge(wprep_pe, 1)
                dve.tensor_copy(wg1_t[:, :], misc_ps[0:16, 0:P]).then_inc(wprep, 1)
                dve.tensor_copy(wall[:, CR:CR + EXPERTS], misc_ps[:, P:P + EXPERTS]).then_inc(wprep, 1)
                dve.tensor_copy(bias[:, :], misc_ps[:, 2 * P:3 * P]).then_inc(wprep, 1)
                dve.wait_ge(wprep, 5)
                vv = wall[:, CV:CV + P].rearrange("p (h v) -> p h v", v=DV)
                dve.scalar_tensor_tensor(out=vv, in0=vmean[:, :].rearrange("p (h a) -> p h a", a=1).broadcast_to([P, HEADS, DV]),
                                         scalar=-1.0 / DV, in1=vv, op0=ALU.mult, op1=ALU.add).then_inc(wprep, 1)
                dve.wait_ge(wprep_pe, 2)
                dve.tensor_copy(wall[:, CG:CG + KW], misc_ps[:, 3 * P:3 * P + KW]).then_inc(wprep, 1)
                dve.wait_ge(consts, CONSTS)
                for i in range(2):
                    dve.tensor_tensor(decay_sum[i][:, :], tri[i][:, :], first_half[i][:, :], ALU.subtract).then_inc(wprep, 1)
                dve.wait_ge(wprep, 9)
                dve.tensor_copy(wall_hi[:, :], wall[:, :]).then_inc(wprep, 1)
                dve.wait_ge(wprep, 10)
                dve.tensor_tensor(wall_lo[:, :], wall[:, :], wall_hi[:, :], ALU.subtract).then_inc(split_done, 1)

            def layer_norm(n, half, par):
                wait(dve, x_loaded[par], 16 * PIECES * (half + 1))
                wait(dve, ln_step, 3 * n - 1)
                wait(dve, xn_done, n)
                wait(dve, rstd_done, n)
                for j in range(TILES):
                    i = dve.bn_stats(stats[:, j, :], x_in[par][:, j, :])
                i.then_inc(ln_step, 1)
                wait(dve, ln_step, 3 * n + 1)
                dve.sem_inc(dve_past, 1)
                for j in range(TILES):
                    i = dve.bn_aggr(moments[:, j, :], stats[:, j, :])
                i.then_inc(ln_step, 1)
                wait(dve, ln_step, 3 * n + 2)
                dve.tensor_scalar(var_eps[:, :], moments[:, :, 1], EPS, None, ALU.add).then_inc(ln_step, 1)

            def mean_shift(n):
                wait(dve, rstd_done, n + 1)
                wait(dve, xn_done, n)
                dve.scalar_tensor_tensor(out=shift[:, :], in0=moments[:, :, 0], scalar=-1.0, in1=rstd[:, :],
                                         op0=ALU.mult, op1=ALU.mult).then_inc(shift_done, 1)

            def x_low(n, par):
                wait(dve, xt_hi_done, n + 1)
                dve.tensor_tensor(xt_lo[par][:, :], misc_ps[:, :], xt_hi[par][:, :], ALU.subtract).then_inc(xt_lo_done, 1)

            def negative_abs(n, par):
                wait(dve, proj_copied, 4 * n + 4)
                wait(dve, kg_exp_done, n)
                kg = proj[par][:, :, CG:CG + KW]
                dve.scalar_tensor_tensor(out=kg_neg[:, :, :], in0=kg, scalar=-1.0, in1=kg, op0=ALU.mult,
                                         op1=ALU.min).then_inc(kg_neg_done, 1)

            def router(n, par):
                wait(dve, mix_done, n)
                wait(dve, gap_t_done, n)
                dve.sem_inc(dve_past, 1)
                for j in range(TILES):
                    i = dve.max(top[:, j, :], proj[par][:, j, CR:CR + EXPERTS])
                i.then_inc(router_step, 1)
                wait(dve, router_step, 5 * n + 1)
                dve.tensor_tensor(gap[:, :], top[:, :, 1], top[:, :, 0], ALU.subtract).then_inc(gap_done, 1)
                for j in range(TILES):
                    i = dve.max_index(top_no[:, j, :], top[:, j, :], proj[par][:, j, CR:CR + EXPERTS])
                i.then_inc(router_step, 1)
                wait(dve, router_step, 5 * n + 2)
                dve.tensor_copy(top_nof[:, :, :], top_no[:, :, :]).then_inc(router_step, 1)
                wait(dve, router_step, 5 * n + 3)
                for k, pick in enumerate((pick1, pick2)):
                    i = dve.tensor_tensor(pick[:, :, :], expert_no[:, :, :],
                                          top_nof[:, :, k:k + 1].broadcast_to([P, TILES, EXPERTS]), ALU.is_equal)

            def mix_weights(n, par):
                wait(dve, gap_t_done, n + 1)
                dve.tensor_scalar(p1[:, :], gap_t[:, :], -0.5, 0.5, ALU.mult, ALU.add)
                dve.tensor_scalar(p2[:, :], gap_t[:, :], 0.5, 0.5, ALU.mult, ALU.add).then_inc(router_step, 1)
                wait(dve, router_step, 5 * n + 4)
                for pick, pk in ((pick1, p1), (pick2, p2)):
                    i = dve.tensor_tensor(pick[:, :, :], pick[:, :, :],
                                          pk[:, :].rearrange("p (t a) -> p t a", a=1).broadcast_to([P, TILES, EXPERTS]), ALU.mult)
                i.then_inc(router_step, 1)
                wait(dve, router_step, 5 * n + 5)
                wait(dve, added, 8 * (n - 1))
                dve.tensor_tensor(mix[par][:, :, :], pick1[:, :, :], pick2[:, :, :], ALU.add).then_inc(mix_done, 1)

            def log_gate(n, par):
                wait(dve, kg_ln_done, n + 1)
                wait(dve, e_done, 3 * n)
                dve.scalar_tensor_tensor(out=log_g[:, :, :], in0=proj[par][:, :, CG:CG + KW], scalar=0.0,
                                         in1=kg_ln[:, :, :], op0=ALU.min, op1=ALU.subtract).then_inc(log_g_done, 1)

            def carry_decay(b):
                wait(dve, e_done, 3 * b + 3)
                wait(dve, carry_done, 2 * b)
                dve.tensor_tensor(carry_half[:, :, :], e_pos[0:1, 0:TILES:2, :], e_neg[0:1, 1:TILES:2, :],
                                  ALU.mult).then_inc(decayed, 1)
                wait(dve, decayed, 2 * b + 1)
                dve.tensor_tensor(carry_dec[:, :, :], carry_half[:, :, :], g_first[:, :, :],
                                  ALU.mult).then_inc(decayed, 1)

            def carry_on(b, bp, s):
                wait(dve, state_done, 4 * b + s + 1)
                wait(dve, decayed, 2 * b + 2)
                wait(dve, kv_joined, 2 * (b - 1) + s + 1)
                dd = carry_dec[0:1, s, :].rearrange("p (h k a) -> p h k a", h=HEADS, a=1).broadcast_to([1, HEADS, DK, DV])
                dve.tensor_tensor(carry[s][:, :].rearrange("p (h k v) -> p h k v", h=HEADS, k=DK),
                                  state_ps[0:1, :].rearrange("p (h k v) -> p h k v", h=HEADS, k=DK), dd,
                                  ALU.mult).then_inc(carry_done, 1)

            def read_state(b, bp, i):
                j = ORDER[i]
                wait(dve, o_done, 4 * b + i - 1)
                wait(dve, state_done, 4 * b + i + 1)
                wait(dve, q_done, b + 1)
                qq = q_dec[:, j, :].rearrange("p (h k a) -> p h k a", h=HEADS, a=1).broadcast_to([P, HEADS, DK, DV])
                dve.tensor_tensor(qs[i % 2][:, :].rearrange("p (h k v) -> p h k v", h=HEADS, k=DK),
                                  state_ps[:, :].rearrange("p (h k v) -> p h k v", h=HEADS, k=DK), qq,
                                  ALU.mult).then_inc(qs_done, 1)

            def sum_keys(b, bp, i):
                j = ORDER[i]
                wait(dve, qs_done, 4 * b + i + 1)
                if i == 0:
                    wait(dve, o_n_done, b)
                dve.tensor_reduce(o[:, j, :].rearrange("p (h v) -> p h v", h=HEADS),
                                  qs[i % 2][:, :].rearrange("p (h k v) -> p h v k", h=HEADS, k=DK), AX_X,
                                  ALU.add).then_inc(o_done, 1)

            def head_var(b):
                wait(dve, o_sq_done, b + 1)
                wait(dve, o_ln_done, b)
                dve.tensor_reduce(o_var[:, :], o_sq[:, :, :].rearrange("p t (h v) -> p (t h) v", v=DV), AX_X,
                                  ALU.add).then_inc(o_var_done, 1)
                wait(dve, o_var_done, b + 1)
                dve.tensor_scalar(o_ve[:, :], o_var[:, :], 4.0 / DV, 4.0 * EPS, ALU.mult,
                                  ALU.add).then_inc(o_ve_done, 1)

            def gate_silu(b):
                wait(dve, gate_t_done, b + 1)
                wait(dve, go_done, b)
                dve.scalar_tensor_tensor(out=gate[:, :, :], in0=gate_t[:, :, :], scalar=1.0, in1=gate_in[:, :, :],
                                         op0=ALU.add, op1=ALU.mult).then_inc(gate_done, 1)

            def gated(b):
                wait(dve, o_r_done, b + 1)
                wait(dve, go_done, b)
                dve.tensor_tensor(o_n[:, :, :].rearrange("p t (h v) -> p (t h) v", v=DV),
                                  o[:, :, :].rearrange("p t (h v) -> p (t h) v", v=DV),
                                  o_r[:, :].rearrange("p (h a) -> p h a", a=1).broadcast_to([P, TILES * HEADS, DV]),
                                  ALU.mult).then_inc(o_n_done, 1)

            def low(b, e):
                wait(dve, down_done, 8 * b + e - 3)
                wait(dve, gelu_done, 16 * b + 2 * e + 1)
                dve.tensor_tensor(h_lo[e % 4][0][:, :], h_act[e % 2][0][:, :], h_hi[e % 4][0][:, :],
                                  ALU.subtract).then_inc(lo_done[0], 1)

            def add_expert(b, bp, e):
                wait(dve, down_done, 8 * b + e + 1)
                if e == 0:
                    wait(dve, mix_done, b + 1)
                    wait(dve, fin1_done, b - 1)
                else:
                    wait(dve, added, 8 * b + e)
                for j in range(TILES):
                    y, w = y_ps[e % 2][:, j * P:(j + 1) * P], mix[bp][:, j, e:e + 1]
                    if e == 0:
                        i = dve.tensor_scalar(acc[bp][:, j, :], y, w, None, ALU.mult)
                    else:
                        i = dve.scalar_tensor_tensor(out=acc[bp][:, j, :], in0=y, scalar=w, in1=acc[bp][:, j, :],
                                                     op0=ALU.mult, op1=ALU.add)
                i.then_inc(added, 1)

            def finish(b, bh, bp):
                wait(dve, fin1_done, b + 1)
                wait(dve, sil_done, b + 1)
                wait(dve, out_done, b)
                dve.scalar_tensor_tensor(out=fin2[:, :], in0=sil_t[:, :], scalar=1.0, in1=fin1[:, :], op0=ALU.add,
                                         op1=ALU.mult).then_inc(fin2_done, 1)
                wait(dve, fin2_done, b + 1)
                wait(dve, res_loaded[bp], 16 * PIECES * (bh + 1))
                wait(dve, stored[bp], 16 * PIECES * bh)
                dve.scalar_tensor_tensor(out=y_out[bp][:, :, :].rearrange("p t d -> p (t d)"), in0=fin2[:, :],
                                         scalar=0.5, in1=x_res[bp][:, :, :].rearrange("p t d -> p (t d)"),
                                         op0=ALU.mult, op1=ALU.add).then_inc(out_done, 1)

            def phase(at):
                for e in range(EXPERTS):
                    if at(1) and e == 6:
                        negative_abs(at(1)[0], at(1)[2])
                    if at(-1) and e == 6:
                        head_var(at(-1)[0])
                    if at(0) and e >= 4:
                        add_expert(at(0)[0], at(0)[2], e - 4)
                    if at(-1) and e < 4:
                        add_expert(at(-1)[0], at(-1)[2], EXPERTS - 4 + e)
                    if at(0) and e == 7:
                        carry_decay(at(0)[0])
                    if at(2) and e == 7:
                        x_low(at(2)[0], at(2)[2])
                    if at(-1) and e in STATE_SLOTS and e > 0:
                        m, mh, mp = at(-1)
                        i = STATE_SLOTS.index(e)
                        if i < 2:
                            carry_on(m, mp, i)
                        read_state(m, mp, i)
                    if at(0):
                        low(at(0)[0], e)
                    if at(-1) and e == 0:
                        carry_on(at(-1)[0], at(-1)[2], 0)
                        read_state(at(-1)[0], at(-1)[2], 0)
                    if at(0) and e == 1:
                        log_gate(at(0)[0], at(0)[2])
                        mix_weights(at(0)[0], at(0)[2])
                    if at(2) and e == 1:
                        layer_norm(*at(2))
                    if at(2) and e == 3:
                        mean_shift(at(2)[0])
                    if e == 4 and not at(1) and at(2):
                        split_small()
                    if at(-2) and e == 4:
                        finish(*at(-2))
                    if at(-1):
                        m, mh, mp = at(-1)
                        if e in STATE_SLOTS:
                            sum_keys(m, mp, STATE_SLOTS.index(e))
                        if e == 5:
                            gate_silu(m)
                        if e == 7:
                            gated(m)
                    if at(1):
                        n, half, par = at(1)
                        if e == 6:
                            router(n, par)
                        if e == 4 and not at(0):
                            dve.wait_ge(w1_high, 1)
                            dve.tensor_tensor(w1_lo[:, :, :], w1_raw[:, :, :], w1_hi[:, :, :],
                                              ALU.subtract).then_inc(w1_split, 1)

            phases(dve, phase)

        @block.tensor
        def _(pe):
            pe.wait_ge(consts, CONSTS)
            pe.wait_ge(ones_made, 1)
            pe.wait_ge(w_small, 16 * 9)
            pe.transpose(misc_ps[0:16, 0:P], wg1_in[:, :], ident[:, :])
            pe.transpose(misc_ps[:, P:P + EXPERTS], router_in[:, :], ident[0:EXPERTS, 0:EXPERTS])
            pe.matmul(misc_ps[:, 2 * P:3 * P], ones_row[:, :], bg_row[:, :], start=True, stop=True).then_inc(wprep_pe, 1)
            pe.wait_ge(wprep, 5)
            pe.matmul(misc_ps[:, 3 * P:3 * P + KW], wg1_t[:, :], wg2_in[:, :], start=True, stop=True).then_inc(wprep_pe, 1)
            pe.wait_ge(wprep, 7)

            def three(dst, a_hi, a_lo, b_hi, b_lo, start=True, stop=True):
                pe.matmul(dst, a_hi, b_hi, start=start, stop=False)
                pe.matmul(dst, a_hi, b_lo, start=False, stop=False)
                return pe.matmul(dst, a_lo, b_hi, start=False, stop=stop)

            def up(b, bp, e):
                if e == 0:
                    wait(pe, xt_lo_done, b + 1)
                    if isinstance(b, int) and b == 0:
                        pe.wait_ge(w1_split, 1)
                        pe.wait_ge(proj_copied, 4)
                for f in range(FH):
                    wait(pe, gelu_done, 16 * b + 2 * e + f - 3)
                    c = slice(f * P, (f + 1) * P)
                    three(h_ps[e % 2 * 2 + f][:, :], w1_hi[:, e, c], w1_lo[:, e, c], xt_hi[bp][:, :],
                          xt_lo[bp][:, :]).then_inc(up_done, 1)

            def down(b, e):
                if isinstance(b, int) and b == 0 and e == 0:
                    pe.wait_ge(w2_split, 1)
                wait(pe, lo_done[0], 8 * b + e + 1)
                wait(pe, lo_done[1], 8 * b + e + 1)
                wait(pe, added, 8 * b + e - 1)
                for j in range(TILES):
                    c = slice(j * P, (j + 1) * P)
                    for f in range(FH):
                        i = three(y_ps[e % 2][:, c], h_hi[e % 4][f][:, c], h_lo[e % 4][f][:, c], w2_hi[:, e, f, :],
                                  w2_lo[:, e, f, :], start=(f == 0), stop=(f == FH - 1))
                i.then_inc(down_done, 1)

            def project(n, par, i):
                j = ORDER[i]
                if isinstance(n, int) and n == 0:
                    pe.wait_ge(split_done, 1)
                if i == 0:
                    wait(pe, xt_lo_done, n + 1)
                elif proj_bank(n, i) is misc_ps:
                    wait(pe, proj_copied, 4 * n + i)
                if i == 2:
                    wait(pe, attn_done, n - 2)
                c = slice(j * P, (j + 1) * P)
                three(proj_bank(n, i)[:, 0:CW], xt_hi[par][:, c], xt_lo[par][:, c], wall_hi[:, :],
                      wall_lo[:, :]).then_inc(proj_done, 1)

            def states(b, i):
                wait(pe, kv_done, 4 * b + i + 1)
                wait(pe, qs_done, 4 * b + i)
                if i < 2:
                    pe.matmul(state_ps[:, :], tri[0][:, :], kv[ORDER[i]][:, :], start=True, stop=True).then_inc(state_done, 1)
                else:
                    wait(pe, kv_joined, 2 * b + i - 1)
                    pe.matmul(state_ps[:, :], tri[1][:, :], kv[ORDER[i]][:, :], start=True, stop=True).then_inc(state_done, 1)

            def decay(b, last):
                wait(pe, log_g_done, b + 1)
                if last:
                    wait(pe, attn_done, b - 1)
                else:
                    wait(pe, proj_copied, 4 * b + 8)
                for c in range(2):
                    dst = misc_ps[:, 0:TILES * KW].rearrange("p (t k) -> p t k", k=KW)[:, c:TILES:2, :]
                    i = pe.matmul(dst, decay_sum[c][:, :], log_g[:, c:TILES:2, :], start=True, stop=True)
                i.then_inc(decay_done, 1)

            def phase(at):
                for e in range(EXPERTS):
                    if at(0):
                        b = at(0)[0]
                        up(b, at(0)[2], e)
                    if at(0) and e >= 3:
                        down(b, e - 3)
                    if at(-1) and e < 3:
                        down(at(-1)[0], EXPERTS - 3 + e)
                    if at(-1) and e in STATE_SLOTS:
                        states(at(-1)[0], STATE_SLOTS.index(e))
                    if at(0) and e == 6:
                        decay(b, not at(1))
                    if at(2) and e == 7:
                        n, half, par = at(2)
                        wait(pe, xn_done, n + 1)
                        wait(pe, e_done, 3 * (n - 1))
                        if isinstance(n, int) and n == 1:
                            wait(pe, proj_copied, 4)
                        for j in range(TILES):
                            i = pe.transpose(misc_ps[:, j * P:(j + 1) * P], xn[:, j, :], ident[:, :])
                        i.then_inc(xt_turned, 1)
                    if at(-2):
                        m2 = at(-2)[0]
                        if e == 2:
                            wait(pe, go_done, m2 + 1)
                            if at(1):
                                wait(pe, proj_copied, 4 * m2 + 14)
                            elif at(-1):
                                wait(pe, e_done, 3 * (m2 + 2))
                            else:
                                wait(pe, attn_done, m2)
                            for j in range(TILES):
                                i = pe.transpose(misc_ps[:, j * P:(j + 1) * P], go[:, j, :], ident[:, :])
                            i.then_inc(go_turned, 1)
                        if e == 3:
                            wait(pe, go_t_done, m2 + 1)
                            for j in range(TILES):
                                c = slice(j * P, (j + 1) * P)
                                i = pe.matmul(misc_ps[:, c], go_t[:, c], wo[:, :], start=True, stop=True)
                            i.then_inc(wo_done, 1)
                    if at(1) and e in PROJ_SLOTS:
                        project(at(1)[0], at(1)[2], PROJ_SLOTS.index(e))

            phases(pe, phase)


_INS = ['L0_attn_inputs', 'L0_attn_Wq', 'L0_attn_Wk', 'L0_attn_Wg1', 'L0_attn_Wg2', 'L0_attn_Wv', 'L0_attn_Wg',
        'L0_attn_bg', 'L0_attn_Wo', 'L0_ffn_router_w', 'L0_ffn_w1', 'L0_ffn_w2']
_OUTS = [((32, 256, 128), 'float32')]


def kernel(**inputs):
    import numpy as _np
    import concourse.bacc as _bacc
    from concourse import mybir as _mybir
    from concourse.bass_utils import run_bass_kernel_spmd as _run

    nc = _bacc.Bacc("TRN2", target_bir_lowering=False, num_devices=1)
    arrays, args = {}, []
    for name in _INS:
        a = _np.ascontiguousarray(inputs[name])
        arrays[f"in_{name}_dram"] = a
        args.append(nc.dram_tensor(f"in_{name}_dram", a.shape, _mybir.dt.from_np(a.dtype), kind="ExternalInput").ap())
    for i, (shape, dtype) in enumerate(_OUTS):
        dt = _mybir.dt.from_np(_np.dtype(dtype))
        args.append(nc.dram_tensor(f"out_{i}_dram", shape, dt, kind="ExternalOutput").ap())
    gla_moe_kernel(nc, *args)
    r = _run(nc, [arrays], core_ids=[0])
    got = tuple(r.results[0][f"out_{i}_dram"] for i in range(len(_OUTS)))
    return got[0]
```
